# Optimizing a Trainium2 kernel written in Bass

```python
import numpy as np
import jax
import jax.numpy as jnp

def _softmax(x, axis=-1):
    return jax.nn.softmax(x, axis=axis)

def _gelu(x):
    return jax.nn.gelu(x, approximate=True)

def _silu(x):
    return jax.nn.silu(x)

def _sigmoid(x):
    return jax.nn.sigmoid(x)

def _layernorm(x, axis=-1, eps=1e-05):
    m = jnp.mean(x, axis=axis, keepdims=True)
    v = jnp.var(x, axis=axis, keepdims=True)
    return (x - m) / jnp.sqrt(v + eps)

def _scatter_add(tgt, idx, src, axis=0):
    return tgt.at[idx].add(src)

def _segment_sum(src, seg, n):
    return jax.ops.segment_sum(src, seg, n)
kernel_name = 'mk_prb_d1_jaxref_r8_45b23d'

def setup_inputs(seed: int=0):
    np.random.seed(seed)
    _w = jnp.asarray

    def _L0_attn_setup():
        import jax, jax.numpy as jnp
        import numpy as np
        B, T, C, H = (2, 256, 256, 16)
        D = C // H

        def _rope(x):
            t = x.shape[-2]
            d = x.shape[-1]
            freqs = jnp.arange(0, d, 2, dtype=jnp.float32) / d
            angles = jnp.arange(t, dtype=jnp.float32)[:, None] * freqs[None, :]
            emb = jnp.concatenate([jnp.sin(angles), jnp.cos(angles)], axis=-1)
            return x * emb
        key = jax.random.key(seed)
        k0, k1, k2, k3, k4 = jax.random.split(key, 5)
        s = 1.0 / np.sqrt(C)
        x = jax.random.normal(k0, (B, T, C), dtype=jnp.float32)
        qkv_w = jax.random.normal(k1, (3 * C, C), dtype=jnp.float32) * s
        qkv_b = jax.random.normal(k2, (3 * C,), dtype=jnp.float32) * s
        out_w = jax.random.normal(k3, (C, C), dtype=jnp.float32) * s
        out_b = jax.random.normal(k4, (C,), dtype=jnp.float32) * s
        return {'x': x, 'qkv_w': qkv_w, 'qkv_b': qkv_b, 'out_w': out_w, 'out_b': out_b}
    _L0_attn_in = _L0_attn_setup()

    def _L0_ffn_setup():
        import jax, jax.numpy as jnp
        import numpy as np
        BLOCK_SIZE = 32
        HIDDEN_SIZE = 256
        MLP_DIM = 2048
        NVFP4_LUT = jnp.array([0.0, 0.5, 1.0, 1.5, 2.0, 3.0, 4.0, 6.0, 0.0, -0.5, -1.0, -1.5, -2.0, -3.0, -4.0, -6.0], dtype=jnp.float32)

        def dequant_nvfp4(W_packed, scales, block=BLOCK_SIZE):
            N = W_packed.shape[0]
            low = W_packed & 15
            high = W_packed >> 4 & 15
            idx = jnp.stack([low, high], axis=-1).reshape(N, -1)
            vals = NVFP4_LUT[idx]
            K = vals.shape[1]
            vals = vals.reshape(N, K // block, block) * scales[:, :, None]
            return vals.reshape(N, K)
        key = jax.random.key(seed)
        ks = jax.random.split(key, 7)
        x = jax.random.normal(ks[0], (4, 32, HIDDEN_SIZE), dtype=jnp.float32)
        gate_W_packed = jax.random.randint(ks[1], (MLP_DIM, HIDDEN_SIZE // 2), 0, 32, dtype=jnp.int32)
        gate_scales = jax.random.uniform(ks[2], (MLP_DIM, HIDDEN_SIZE // BLOCK_SIZE), dtype=jnp.float32) * 0.1 + 0.001
        up_W_packed = jax.random.randint(ks[3], (MLP_DIM, HIDDEN_SIZE // 2), 0, 32, dtype=jnp.int32)
        up_scales = jax.random.uniform(ks[4], (MLP_DIM, HIDDEN_SIZE // BLOCK_SIZE), dtype=jnp.float32) * 0.1 + 0.001
        down_W_packed = jax.random.randint(ks[5], (HIDDEN_SIZE, MLP_DIM // 2), 0, 32, dtype=jnp.int32)
        down_scales = jax.random.uniform(ks[6], (HIDDEN_SIZE, MLP_DIM // BLOCK_SIZE), dtype=jnp.float32) * 0.1 + 0.001
        return {'x': x, 'gate_W_packed': gate_W_packed, 'gate_scales': gate_scales, 'up_W_packed': up_W_packed, 'up_scales': up_scales, 'down_W_packed': down_W_packed, 'down_scales': down_scales}
    _L0_ffn_in = _L0_ffn_setup()
    _d = {'L0_attn_x': _L0_attn_in['x'], 'L0_attn_qkv_w': _L0_attn_in['qkv_w'], 'L0_attn_qkv_b': _L0_attn_in['qkv_b'], 'L0_attn_out_w': _L0_attn_in['out_w'], 'L0_attn_out_b': _L0_attn_in['out_b'], 'L0_ffn_gate_W_packed': _L0_ffn_in['gate_W_packed'], 'L0_ffn_gate_scales': _L0_ffn_in['gate_scales'], 'L0_ffn_up_W_packed': _L0_ffn_in['up_W_packed'], 'L0_ffn_up_scales': _L0_ffn_in['up_scales'], 'L0_ffn_down_W_packed': _L0_ffn_in['down_W_packed'], 'L0_ffn_down_scales': _L0_ffn_in['down_scales']}
    _x0 = _d['L0_attn_x']
    _d['L0_attn_x'] = jax.random.normal(jax.random.fold_in(jax.random.key(seed), 1), (16, 256, 256), dtype=_x0.dtype)
    del _x0
    return _d

def reference(L0_attn_x, L0_attn_qkv_w, L0_attn_qkv_b, L0_attn_out_w, L0_attn_out_b, L0_ffn_gate_W_packed, L0_ffn_gate_scales, L0_ffn_up_W_packed, L0_ffn_up_scales, L0_ffn_down_W_packed, L0_ffn_down_scales):

    def _L0_attn_ref(x, qkv_w, qkv_b, out_w, out_b):
        import jax, jax.numpy as jnp
        import numpy as np
        B, T, C, H = (2, 256, 256, 16)
        D = C // H

        def _rope(x):
            t = x.shape[-2]
            d = x.shape[-1]
            freqs = jnp.arange(0, d, 2, dtype=jnp.float32) / d
            angles = jnp.arange(t, dtype=jnp.float32)[:, None] * freqs[None, :]
            emb = jnp.concatenate([jnp.sin(angles), jnp.cos(angles)], axis=-1)
            return x * emb
        b, t, c = x.shape
        qkv = x @ qkv_w.T + qkv_b
        qkv = qkv.reshape(b, t, 3, H, D)
        q = jnp.transpose(qkv[:, :, 0], (0, 2, 1, 3))
        k = jnp.transpose(qkv[:, :, 1], (0, 2, 1, 3))
        v = jnp.transpose(qkv[:, :, 2], (0, 2, 1, 3))
        q = _rope(q)
        k = _rope(k)
        scores = jnp.einsum('bhqd,bhkd->bhqk', q, k) / np.sqrt(D)
        causal = jnp.tril(jnp.ones((t, t), dtype=bool))
        scores = jnp.where(causal, scores, -jnp.inf)
        attn = jax.nn.softmax(scores, axis=-1)
        out = jnp.einsum('bhqk,bhkd->bqhd', attn, v).reshape(b, t, c)
        return out @ out_w.T + out_b

    def _L0_ffn_ref(x, gate_W_packed, gate_scales, up_W_packed, up_scales, down_W_packed, down_scales):
        import jax, jax.numpy as jnp
        import numpy as np
        BLOCK_SIZE = 32
        HIDDEN_SIZE = 256
        MLP_DIM = 2048
        NVFP4_LUT = jnp.array([0.0, 0.5, 1.0, 1.5, 2.0, 3.0, 4.0, 6.0, 0.0, -0.5, -1.0, -1.5, -2.0, -3.0, -4.0, -6.0], dtype=jnp.float32)

        def dequant_nvfp4(W_packed, scales, block=BLOCK_SIZE):
            N = W_packed.shape[0]
            low = W_packed & 15
            high = W_packed >> 4 & 15
            idx = jnp.stack([low, high], axis=-1).reshape(N, -1)
            vals = NVFP4_LUT[idx]
            K = vals.shape[1]
            vals = vals.reshape(N, K // block, block) * scales[:, :, None]
            return vals.reshape(N, K)
        B, S, H = x.shape
        xt = x.reshape(B * S, H)
        Wg = dequant_nvfp4(gate_W_packed, gate_scales)
        Wu = dequant_nvfp4(up_W_packed, up_scales)
        Wd = dequant_nvfp4(down_W_packed, down_scales)
        gate = jnp.einsum('th,nh->tn', xt, Wg)
        up = jnp.einsum('th,nh->tn', xt, Wu)
        gelu = jnp.tanh(0.7978845608028654 * (gate + 0.044715 * gate ** 3)) * gate * 0.5 + gate * 0.5
        inter = gelu * up
        out = jnp.einsum('tn,hn->th', inter, Wd)
        return out.reshape(B, S, H)
    x = L0_attn_x
    xn = _layernorm(x, axis=-1)
    x = x + _L0_attn_ref(xn, L0_attn_qkv_w, L0_attn_qkv_b, L0_attn_out_w, L0_attn_out_b) + _L0_ffn_ref(xn, L0_ffn_gate_W_packed, L0_ffn_gate_scales, L0_ffn_up_W_packed, L0_ffn_up_scales, L0_ffn_down_W_packed, L0_ffn_down_scales)
    return x

_drawn_inputs = setup_inputs


def setup_inputs(seed=0):
    import zlib

    import numpy as np

    out = dict(_drawn_inputs(seed))
    spreads = {}
    factors = {'L0_attn_qkv_w': 4.573, 'L0_attn_qkv_b': 8.0, 'L0_attn_out_w': 4.071, 'L0_attn_out_b': 8.0}
    for name, (base, spread) in spreads.items():
        noise = np.random.default_rng([zlib.crc32(name.encode()), seed]).standard_normal(out[name].shape)
        drawn = base * np.exp(spread * noise) if base else spread * noise
        out[name] = jnp.asarray(drawn.astype(out[name].dtype))
    for name, factor in factors.items():
        out[name] = (out[name] * factor).astype(out[name].dtype)
    return out
```

```python
from contextlib import ExitStack

import numpy as np

import concourse.bass as bass
from concourse import mybir

F32 = mybir.dt.float32
F16 = mybir.dt.float16
BF16 = mybir.dt.bfloat16
I32 = mybir.dt.int32
ALU = mybir.AluOpType
ACT = mybir.ActivationFunctionType

P = 128
B, T, C, H = 16, 256, 256, 16
D = C // H
NTOK = B * T
HID = 2048
BLOCK = 32
EPS = 1e-5
WS = 16.0
CODE = 2.0 ** 14
NEG = -1e30
HP = 20
VW = (H - 1) * HP + 32
HEADS = 4
GROUPS = H // HEADS
FILLS = 3
SLICES = 16
NW = 3 * HID
SW = NW // SLICES
CH = 512
SUB = CH // P
NTILES = HID // P


def build(nc, x, qkv_wT, qkv_b, v_b, out_wT, out_b, codes, scales, emb, mask_q, mask_k, id_f32, id_f16, id_bf16, out):
    ctx = ExitStack()
    with ctx:
        def sb(name, shape, dt):
            return ctx.enter_context(nc.sbuf_tensor(name, shape, dt))

        def sem(name):
            return ctx.enter_context(nc.semaphore(name))

        xT = sb("xT", [P, 2, 2, NTOK], F16)
        attT = sb("attT", [P, 2, 2, NTOK], F16)
        W = sb("W", [P, 2, 2, NW], F16)
        wqkv = sb("wqkv", [P, 2, 2, 3 * C], F16)
        wo = sb("wo", [P, 2, 2, C], F16)
        qs = sb("qs", [P, 2, H, T], F16)
        ks = sb("ks", [P, 2, H, T], F16)
        pT = sb("pT", [P, 2, FILLS, 512], F32)
        V = sb("V", [P, 2, 2, VW], F32)
        qk = sb("qk", [P, 4, T], F32)
        qk16 = sb("qk16", [P, 4, 2, T], F16)
        xs = sb("xs", [P, 2, C], F32)
        xn = sb("xn", [P, 2, C], F32)
        x16 = sb("x16", [P, 2, 2, C], F16)
        oT = sb("oT", [P, 2, 512], F32)
        att = sb("att", [P, 2, C], F32)
        att16 = sb("att16", [P, 2, 2, C], F16)
        emb_sb = sb("emb_sb", [P, T], F32)
        mask_q_sb = sb("mask_q_sb", [P, T], F32)
        mask_k_sb = sb("mask_k_sb", [P, 512], BF16)
        idf = sb("idf", [P, P], F32)
        idh = sb("idh", [P, P], F16)
        idb = sb("idb", [P, P], BF16)
        vb = sb("vb", [P, C], F32)
        qb = sb("qb", [P, 4], F32)
        qb16 = sb("qb16", [P, 4], F32)
        stats = sb("stats", [P, 2, 6], F32)
        moments = sb("moments", [P, 2, 2], F32)
        vareps = sb("vareps", [P, 2], F32)
        rstd = sb("rstd", [P, 2], F32)
        half = sb("half", [P, 2], F32)
        mx = sb("mx", [P, 2, H], F32)
        sh16 = sb("sh16", [P, 2, 2, H], F16)
        shT = sb("shT", [2 * H, T], F16)
        rden = sb("rden", [P, 2, H], F32)
        code = sb("code", [P, SW], I32)
        scale = sb("scale", [P, SW], F32)
        sign = sb("sign", [P, 2, SW], I32)
        wbits = sb("wbits", [P, 2, SW], I32)

        wstage = pT[:, :, :, :].rearrange("p a b c -> p (a b c)")
        wqkv_in = wstage[:, 0:6 * C].rearrange("p (a n) -> p a n", a=2)
        wo_in = wstage[:, 6 * C:8 * C].rearrange("p (a n) -> p a n", a=2)
        qs_f = qs[:, :, :, :].rearrange("p a h t -> p (a h t)")
        ks_f = ks[:, :, :, :].rearrange("p a h t -> p (a h t)").bitcast(F32)
        gel = qs_f[:, 0:2048].bitcast(F32).rearrange("p (b n) -> p b n", b=2)
        inter = qs_f[:, 2048:4096].bitcast(F32).rearrange("p (b n) -> p b n", b=2)
        inter16 = qs_f[:, 4096:6144].rearrange("p (b s n) -> p b s n", b=2, s=2)
        ob = qs_f[:, 6144:6144 + 2 * C].bitcast(F32)
        xres = ks_f[:, 0:2048].rearrange("p (b s c) -> p b s c", b=2, s=SUB)
        res = ks_f[:, 2048:4096].rearrange("p (b s c) -> p b s c", b=2, s=SUB)

        bank = [ctx.enter_context(nc.psum_tensor(f"bank{n}", [P, 512], F32)) for n in range(8)]
        bX, bO, bP, bPV = bank[0], bank[1], bank[2], bank[3]
        bA, bB = bank[4:6], bank[6:8]
        bX16 = bX[:, :].bitcast(F16)
        bO16 = bO[:, :].bitcast(F16)
        bG, bU, bOut = bA, bB, [bX, bP]

        stack = nc.dram_tensor("stack", [2, 2, 2, D, H, T], F16).ap()

        const_in, wts_in, x_in, codes_in = sem("const_in"), sem("wts_in"), sem("x_in"), sem("codes_in")
        stack_out = sem("stack_out")
        stack_in = [[sem(f"stack_in{v}{hf}") for hf in range(2)] for v in range(2)]
        shift_in, ob_in = sem("shift_in"), sem("ob_in")
        xres_in = [sem("xres_in0"), sem("xres_in1")]
        out_done = [sem("out_done0"), sem("out_done1")]
        filled, queries_zero, half_ready, w_high, w_low = (
            sem("filled"), sem("queries_zero"), sem("half_ready"), sem("w_high"), sem("w_low"))
        stats_done, moments_ready, eps_added, rstd_ready = (
            sem("stats_done"), sem("moments_ready"), sem("eps_added"), sem("rstd_ready"))
        xn_ready, x_high, x_low, xT_ready, xT_kept = (
            sem("xn_ready"), sem("x_high"), sem("x_low"), sem("xT_ready"), sem("xT_kept"))
        proj_ready, rope_done, qk_high, qk_low = sem("proj_ready"), sem("rope_done"), sem("qk_high"), sem("qk_low")
        v_ready, v_kept = sem("v_ready"), sem("v_kept")
        scores_ready, max_taken, shift_split = sem("scores_ready"), sem("max_taken"), sem("shift_split")
        shT_ready, shT_kept, rows_zeroed = sem("shT_ready"), sem("shT_kept"), sem("rows_zeroed")
        shifted_ready, exp_done, pv_done, oT_kept = (
            sem("shifted_ready"), sem("exp_done"), sem("pv_done"), sem("oT_kept"))
        o_ready, rden_ready, o_taken, att_high, att_low = (
            sem("o_ready"), sem("rden_ready"), sem("o_taken"), sem("att_high"), sem("att_low"))
        attT_ready, attT_kept = sem("attT_ready"), sem("attT_kept")
        bits_step, bits_ready, scale_ready, wf_ready, wf_high, wf_low = (
            sem("bits_step"), sem("bits_ready"), sem("scale_ready"), sem("wf_ready"), sem("wf_high"), sem("wf_low"))
        gate_ready, up_ready, gelu_done, inter_ready, inter_high, inter_low = (
            sem("gate_ready"), sem("up_ready"), sem("gelu_done"), sem("inter_ready"), sem("inter_high"), sem("inter_low"))
        down_done, acc_taken, xres_ready = (
            sem("down_done"), sem("acc_taken"), sem("xres_ready"))

        block = ctx.enter_context(nc.Block())

        FIRST, LOOP, LAST = -3, (3, 13), B + 2

        def pipeline(eng, step):
            def fixed(i):
                step(i, i % 2, lambda lag: 0 <= i + lag < B)
            for i in range(FIRST, LOOP[0]):
                fixed(i)
            with eng.Fori(0, (LOOP[1] - LOOP[0]) // 2) as j:
                for u in (0, 1):
                    step(j * 2 + (LOOP[0] + u), (LOOP[0] + u) % 2, lambda lag: True)
            for i in range(LOOP[1], LAST):
                fixed(i)

        def wait_apart(eng, semaphore, value):
            if not isinstance(value, int):
                value = eng.to_reg(value)
                eng.wait_ge(semaphore, 1)
            eng.wait_ge(semaphore, value)

        def early(i, lag, n):
            return isinstance(i, int) and i + lag < n

        @block.sync
        def _(sp):
            for dst, src in ((emb_sb, emb), (mask_q_sb, mask_q), (mask_k_sb, mask_k), (idf, id_f32), (idh, id_f16),
                             (idb, id_bf16), (qb, qkv_b)):
                sp.dma_start(dst[:, :], src).then_inc(const_in, 16)
            sp.dma_start(vb[:, :], v_b.partition_broadcast(P)).then_inc(const_in, 16)
            sp.dma_start(wqkv_in, qkv_wT).then_inc(wts_in, 16)
            sp.dma_start(wo_in, out_wT).then_inc(wts_in, 16)

            def step(i, u, live):
                if live(3):
                    b = i + 3
                    if not early(i, 3, 1):
                        sp.wait_ge(xn_ready, b)
                    sp.dma_start(xs[:, :, :], x[bass.ds(b * 2, 2)].rearrange("a p c -> p a c")).then_inc(x_in, 16)
                if live(0):
                    if not early(i, 0, 1):
                        sp.wait_ge(bits_ready, i)
                        sp.wait_ge(wf_ready, i)
                    sp.dma_start(code[:, :], codes[:, bass.ds(i * SW, SW)]).then_inc(codes_in, 16)
                    s0 = scales[:, bass.ds(i * SW, SW)]
                    src = bass.AP(s0.tensor, s0.offset, [[NW, P // 16], [0, 16], [1, SW]])
                    sp.dma_start(scale[:, :], src).then_inc(codes_in, 16)
                if live(-1):
                    sp.wait_ge(shT_kept, i)
                    for part in range(2):
                        r = 4 * D + part
                        sp.dma_start(qs[r:r + 1, 1 - u, :, :], shT[part * H:(part + 1) * H, :]).then_inc(shift_in, 16)
                if live(1):
                    b = i + 1
                    v = 1 - u
                    sp.wait_ge(qk_high, b + 1)
                    sp.wait_ge(qk_low, b + 1)
                    for f in range(4):
                        for part in range(2):
                            h0 = 8 * (f % 2)
                            dst = stack[v, f // 2, part].rearrange("d h t -> h d t")[h0:h0 + 8]
                            sp.dma_start(dst, qk16[:, f, part, :]).then_inc(stack_out, 16)
                    sp.wait_ge(stack_out, (b + 1) * 128)
                    for hf in range(2):
                        if not early(i, 1, 2):
                            sp.wait_ge(shifted_ready, (b - 2) * (GROUPS * FILLS) + 6 * (hf + 1))
                        hs = slice(8 * hf, 8 * hf + 8)
                        q0 = stack[v, 0, :, :, hs, :]
                        k0 = stack[v, 1, :, :, hs, :]
                        n = 8 * T
                        src = bass.AP(q0.tensor, q0.offset, [[0, 2], [H * T, 2 * D], [1, n]])
                        sp.dma_start(qs[0:4 * D, v, hs, :].rearrange("p h t -> p (h t)"), src).then_inc(stack_in[v][hf], 16)
                        for part in range(2):
                            src = bass.AP(k0.tensor, k0.offset + part * D * H * T, [[0, 2], [H * T, D], [1, n]])
                            dst = ks[2 * part * D:2 * (part + 1) * D, v, hs, :].rearrange("p h t -> p (h t)")
                            sp.dma_start(dst, src).then_inc(stack_in[v][hf], 16)

            pipeline(sp, step)

            sp.wait_ge(pv_done, B * GROUPS)
            sp.dma_start(ob, out_b.partition_broadcast(P)).then_inc(ob_in, 16)
            xc = x.rearrange("(k s) p c -> k p s c", s=SUB)
            oc = out.rearrange("(k s) p c -> k p s c", s=SUB)
            for k in range(2):
                sp.dma_start(xres[:, k], xc[k]).then_inc(xres_in[k], 16)

            def store(k, u):
                sp.wait_ge(acc_taken, (k + 1) * 2)
                sp.dma_start(oc[k] if isinstance(k, int) else oc[bass.ds(k, 1)].rearrange("k p s c -> p (k s) c"),
                             res[:, u]).then_inc(out_done[u], 16)

            with sp.Fori(0, NTOK // CH // 2 - 1) as j:
                for u in range(2):
                    store(j * 2 + u, u)
                    sp.dma_start(xres[:, u], xc[bass.ds(j * 2 + (2 + u), 1)].rearrange("k p s c -> p (k s) c"))\
                      .then_inc(xres_in[u], 16)
            for u in range(2):
                store(NTOK // CH - 2 + u, u)
            for u in range(2):
                sp.wait_ge(out_done[u], NTOK // CH // 2 * 16)

        @block.gpsimd
        def _(pool):
            nc.gpsimd.memset(qs[64:128, :, :, :].bitcast(F32), 0.0).then_inc(queries_zero, 1)
            pool.wait_ge(queries_zero, 1)
            nc.gpsimd.memset(half[:, :], -0.5).then_inc(half_ready, 1)

            def step(i, u, live):
                if live(-1):
                    wait_apart(pool, codes_in, i * 32)
                    nc.gpsimd.tensor_scalar(scale[:, :], scale[:, :], CODE * WS, None, ALU.mult).then_inc(scale_ready, 1)
                    pool.wait_ge(scale_ready, i)
                    pool.wait_ge(bits_ready, i)
                    val = wbits[:, :, :].bitcast(F16).rearrange("p a (n e) -> p a n e", e=2)[:, :, :, 0]
                    sc = scale[:, :].unsqueeze(1).broadcast_to([P, 2, SW])
                    nc.gpsimd.tensor_tensor(wbits[:, :, :].bitcast(F32), val, sc, ALU.mult).then_inc(wf_ready, 1)
                if live(1):
                    b = i + 1
                    pool.wait_ge(qk_high, b + 1)
                    if not early(i, 1, 1):
                        pool.wait_ge(stack_out, b * 128)
                    nc.gpsimd.tensor_tensor(qk16[:, :, 1, :], qk[:, :, :], qk16[:, :, 0, :], ALU.subtract)\
                        .then_inc(qk_low, 1)
                if live(-2):
                    for qt in range(2):
                        pool.wait_ge(att_high, (i - 2) * 2 + qt + 1)
                        nc.gpsimd.tensor_tensor(att16[:, qt, 1, :], att[:, qt, :], att16[:, qt, 0, :], ALU.subtract)\
                            .then_inc(att_low, 1)
                if live(-1):
                    pool.wait_ge(wf_high, i)
                    o = bass.ds((i - 1) * SW, SW)
                    nc.gpsimd.tensor_tensor(W[:, :, 1, o], wbits[:, :, :].bitcast(F32), W[:, :, 0, o], ALU.subtract)\
                        .then_inc(wf_low, 1)
                if live(3):
                    b = i + 3
                    wait_apart(pool, moments_ready, b + 1)
                    nc.gpsimd.tensor_scalar(vareps[:, :], moments[:, :, 1], EPS, None, ALU.add).then_inc(eps_added, 1)
                    pool.wait_ge(eps_added, b + 1)
                    if early(i, 3, 1):
                        pool.wait_ge(half_ready, 1)
                    else:
                        pool.wait_ge(xn_ready, b)
                    nc.gpsimd.tensor_tensor(rstd[:, :], vareps[:, :], half[:, :], ALU.pow).then_inc(rstd_ready, 1)
                    pool.wait_ge(x_high, b + 1)
                    nc.gpsimd.tensor_tensor(x16[:, :, 1, :], xn[:, :, :], x16[:, :, 0, :], ALU.subtract)\
                        .then_inc(x_low, 1)
                if live(1) and not early(i, 1, 2):
                    if live(3):
                        pool.wait_ge(x_low, i + 4)
                    elif live(-1):
                        pool.wait_ge(wf_low, i)
                    for hf in range(2):
                        wait_apart(pool, shifted_ready, (i - 1) * (GROUPS * FILLS) + 6 * (hf + 1))
                        nc.gpsimd.memset(qs[64:66, 1 - u, 8 * hf:8 * hf + 8, :].bitcast(F32), 0.0)\
                            .then_inc(rows_zeroed, 1)
                    pool.wait_ge(rows_zeroed, i * 2)

            pipeline(pool, step)

            pool.wait_ge(ob_in, 16)

            def residual(k, u):
                pool.wait_ge(xres_in[u], (k // 2 + 1) * 16 if isinstance(k, int) else (k + 1) * 16)
                nc.gpsimd.tensor_tensor(xres[:, u], xres[:, u], ob.unsqueeze(1).broadcast_to([P, SUB, C]), ALU.add)\
                    .then_inc(xres_ready, 1)

            with pool.Fori(0, NTOK // CH // 2) as j:
                for u in range(2):
                    residual(j + 0, u)

        @block.scalar
        def _(act):
            act.wait_ge(wts_in, 32)
            nc.scalar.activation(wqkv[:, :, 0, :], wqkv_in, ACT.Copy, scale=WS).then_inc(w_high, 1)
            nc.scalar.activation(wo[:, :, 0, :], wo_in, ACT.Copy, scale=WS).then_inc(w_high, 1)

            def exps(i, u, g):
                b = i - 1
                if g < 2 and early(i, -1, 1):
                    act.wait_ge(w_low, 2)
                else:
                    act.wait_ge(pv_done, b * GROUPS + g - 1)
                for f in range(FILLS):
                    act.wait_ge(shifted_ready, (b * GROUPS + g) * FILLS + f + 1)
                    nc.scalar.activation(pT[:, g % 2, f, :], bB[(g * FILLS + f) % 2][:, :], ACT.Exp, scale=D ** -0.5)\
                        .then_inc(exp_done, 1)

            def keep_o(i, hf):
                b = i - 1
                act.wait_ge(pv_done, b * GROUPS + 2 * hf + 2)
                if not early(i, -1, 1):
                    act.wait_ge(o_ready, b * 2)
                nc.scalar.activation(oT[:, hf, :], bPV[:, :], ACT.Copy).then_inc(oT_kept, 1)

            def att_hi(i, qt):
                b = i - 2
                act.wait_ge(o_taken, b * 2 + qt + 1)
                if not early(i, -2, 1):
                    act.wait_ge(attT_ready, b)
                nc.scalar.activation(att16[:, qt, 0, :], att[:, qt, :], ACT.Copy).then_inc(att_high, 1)

            def step(i, u, live):
                if live(2):
                    b = i + 2
                    act.wait_ge(xT_ready, b + 1)
                    nc.scalar.activation(xT[:, :, :, bass.ds(b * T, T)].rearrange("p a s t -> p (a s) t"),
                                         bX16.rearrange("p (a t) -> p a t", a=4), ACT.Copy).then_inc(xT_kept, 1)
                if live(-1):
                    act.wait_ge(shT_ready, i)
                    if not early(i, -1, 1):
                        act.wait_ge(shift_in, (i - 1) * 32)
                    nc.scalar.activation(shT[:, :], bX16[0:2 * H, 0:T], ACT.Copy).then_inc(shT_kept, 1)
                if live(1):
                    b = i + 1
                    act.wait_ge(rope_done, (b + 1) * 2)
                    if not early(i, 1, 1):
                        act.wait_ge(stack_out, b * 128)
                    nc.scalar.activation(qk16[:, :, 0, :], qk[:, :, :], ACT.Copy).then_inc(qk_high, 1)
                if live(-1):
                    exps(i, u, 0)
                    act.wait_ge(wf_ready, i)
                    nc.scalar.activation(W[:, :, 0, bass.ds((i - 1) * SW, SW)], wbits[:, :, :].bitcast(F32), ACT.Copy)\
                        .then_inc(wf_high, 1)
                    exps(i, u, 1)
                if live(-2):
                    att_hi(i, 0)
                if live(-1):
                    exps(i, u, 2)
                    keep_o(i, 0)
                if live(-2):
                    att_hi(i, 1)
                if live(-1):
                    exps(i, u, 3)
                if live(-2):
                    act.wait_ge(attT_ready, i - 1)
                    nc.scalar.activation(attT[:, :, :, bass.ds((i - 2) * T, T)].rearrange("p a s t -> p (a s) t"),
                                         bO16.rearrange("p (a t) -> p a t", a=4), ACT.Copy).then_inc(attT_kept, 1)
                if live(-1):
                    keep_o(i, 1)
                if live(3):
                    b = i + 3
                    act.wait_ge(xn_ready, b + 1)
                    if not early(i, 3, 1):
                        act.wait_ge(xT_ready, b)
                    nc.scalar.activation(x16[:, :, 0, :], xn[:, :, :], ACT.Copy).then_inc(x_high, 1)

            pipeline(act, step)

            def mlp(n, v):
                act.wait_ge(gate_ready, n + 1)
                if not (isinstance(n, int) and n < 2):
                    act.wait_ge(inter_ready, n - 1)
                nc.scalar.activation(gel[:, v], bG[v][:, :], ACT.Gelu_apprx_tanh, scale=1.0 / WS).then_inc(gelu_done, 1)
                act.wait_ge(inter_ready, n + 1)
                if not (isinstance(n, int) and n < 2):
                    act.wait_ge(down_done, n - 1)
                nc.scalar.activation(inter16[:, v, 0, :], inter[:, v, :], ACT.Copy).then_inc(inter_high, 1)

            for n in range(2):
                mlp(n, n)
            with act.Fori(0, NTOK // CH * NTILES // 2 - 1) as j:
                for v in range(2):
                    mlp(j * 2 + (2 + v), v)

        @block.vector
        def _(dve):
            nc.vector.memset(ks[64:128, :, :, :].bitcast(F32), 0.0).then_inc(filled, 1)
            dve.wait_ge(filled, 1)
            nc.vector.memset(ks[64:66, :, :, :], 1.0).then_inc(filled, 1)
            nc.vector.memset(V[:, :, :, :], 0.0).then_inc(filled, 1)
            dve.wait_ge(filled, 3)
            for a in range(2):
                for kt in range(2):
                    nc.vector.memset(V[:, a, kt, D:D + (H - 1) * HP + 1:HP], 1.0).then_inc(filled, 1)
            dve.wait_ge(w_high, 1)
            nc.vector.scalar_tensor_tensor(out=wqkv[:, :, 1, :], in0=wqkv_in, scalar=WS, in1=wqkv[:, :, 0, :],
                                           op0=ALU.mult, op1=ALU.subtract).then_inc(w_low, 1)
            dve.wait_ge(w_high, 2)
            nc.vector.scalar_tensor_tensor(out=wo[:, :, 1, :], in0=wo_in, scalar=WS, in1=wo[:, :, 0, :],
                                           op0=ALU.mult, op1=ALU.subtract).then_inc(w_low, 1)
            dve.wait_ge(const_in, 8 * 16)
            nc.vector.tensor_scalar(qb16[:, :], qb[:, :], WS, None, ALU.mult).then_inc(w_low, 1)
            dve.wait_ge(w_low, 3)

            def rope(i, pair):
                b = i + 1
                dve.wait_ge(proj_ready, b * 2 + pair + 1)
                if pair == 0 and not early(i, 1, 1):
                    dve.wait_ge(qk_low, b)
                for n in range(2):
                    f = 2 * pair + n
                    last = nc.vector.scalar_tensor_tensor(
                        out=qk[:, f, :], in0=bP[:, n * T:(n + 1) * T], scalar=qb16[:, f:f + 1], in1=emb_sb[:, :],
                        op0=ALU.add, op1=ALU.mult)
                last.then_inc(rope_done, 1)

            def row_max(i, g):
                for f in range(FILLS):
                    wait_apart(dve, scores_ready, (i * GROUPS + g) * FILLS + f + 1)
                    s = bA[(g * FILLS + f) % 2]
                    for n in range(HEADS if f == 0 else 2):
                        if f == 0:
                            h, qt, w = HEADS * g + n, 0, P
                        else:
                            h, qt, w = HEADS * g + 2 * (f - 1) + n, 1, T
                        last = nc.vector.tensor_tensor_reduce(
                            s[:, n * w:(n + 1) * w], s[:, n * w:(n + 1) * w], mask_q_sb[:, T - w:T], 1.0, -3e38,
                            ALU.add, ALU.max, mx[:, qt, h:h + 1])
                    last.then_inc(max_taken, 1)

            def normalise(i, qt):
                b = i - 2
                dve.wait_ge(o_ready, b * 2 + qt + 1)
                o = bO[:, :].rearrange("p (h e) -> p h e", e=32)
                nc.vector.reciprocal(rden[:, qt, :], o[:, :, D]).then_inc(rden_ready, 1)
                dve.wait_ge(rden_ready, b * 2 + qt + 1)
                if not early(i, -2, 1):
                    dve.wait_ge(att_low, (b - 1) * 2 + qt + 1)
                nc.vector.tensor_tensor(att[:, qt, :].rearrange("p (h d) -> p h d", d=D), o[:, :, 0:D],
                                        rden[:, qt, :].unsqueeze(2).broadcast_to([P, H, D]), ALU.mult)\
                    .then_inc(o_taken, 1)

            def step(i, u, live):
                if live(1):
                    rope(i, 0)
                if live(0):
                    row_max(i, 0)
                if live(1):
                    rope(i, 1)
                if live(0):
                    dve.wait_ge(v_ready, i + 1)
                    if not early(i, 0, 2):
                        dve.wait_ge(pv_done, (i - 1) * GROUPS)
                    for kt in range(2):
                        dst = V[:, u, kt, 0:H * HP].rearrange("p (h e) -> p h e", e=HP)[:, :, 0:D]
                        last = nc.vector.scalar_tensor_tensor(
                            out=dst, in0=bP[:, kt * C:(kt + 1) * C].rearrange("p (h d) -> p h d", d=D),
                            scalar=1.0 / WS, in1=vb[:, :].rearrange("p (h d) -> p h d", d=D), op0=ALU.mult, op1=ALU.add)
                    last.then_inc(v_kept, 1)
                    row_max(i, 1)
                if live(-2):
                    normalise(i, 0)
                if live(0):
                    row_max(i, 2)
                if live(-2):
                    normalise(i, 1)
                if live(3):
                    b = i + 3
                    dve.wait_ge(x_in, (b + 1) * 16)
                    for tt in range(2):
                        last = nc.vector.bn_stats(stats[:, tt, :], xs[:, tt, :])
                    last.then_inc(stats_done, 1)
                    wait_apart(dve, stats_done, b + 1)
                    for tt in range(2):
                        last = nc.vector.bn_aggr(moments[:, tt, :], stats[:, tt, :])
                    last.then_inc(moments_ready, 1)
                if live(0):
                    row_max(i, 3)
                    dve.wait_ge(max_taken, (i + 1) * (GROUPS * FILLS))
                    if not early(i, 0, 1):
                        dve.wait_ge(shT_ready, i)
                    nc.vector.tensor_scalar(sh16[:, :, 0, :], mx[:, :, :], -1.0, None, ALU.mult).then_inc(shift_split, 1)
                    dve.wait_ge(shift_split, i * 2 + 1)
                    nc.vector.scalar_tensor_tensor(out=sh16[:, :, 1, :], in0=mx[:, :, :], scalar=-1.0,
                                                   in1=sh16[:, :, 0, :], op0=ALU.mult, op1=ALU.subtract)\
                        .then_inc(shift_split, 1)
                    dve.wait_ge(codes_in, (i + 1) * 32)
                    if not early(i, 0, 1):
                        dve.wait_ge(wf_low, i)
                    for par, (m, s) in enumerate(((0x7, 9), (0x70, 5))):
                        nc.vector.tensor_scalar(wbits[:, par, :], code[:, :], m, s, ALU.bitwise_and,
                                                ALU.logical_shift_left)
                        last = nc.vector.tensor_scalar(sign[:, par, :], code[:, :], (8, 128)[par], (12, 8)[par],
                                                       ALU.bitwise_and, ALU.logical_shift_left)
                    last.then_inc(bits_step, 1)
                    dve.wait_ge(bits_step, i + 1)
                    nc.vector.tensor_tensor(wbits[:, :, :], wbits[:, :, :], sign[:, :, :], ALU.bitwise_or)\
                        .then_inc(bits_ready, 1)
                if live(3):
                    b = i + 3
                    dve.wait_ge(rstd_ready, b + 1)
                    if not early(i, 3, 1):
                        dve.wait_ge(x_low, b)
                    for tt in range(2):
                        last = nc.vector.tensor_scalar(xn[:, tt, :], xs[:, tt, :], moments[:, tt, 0:1],
                                                       rstd[:, tt:tt + 1], ALU.subtract, ALU.mult)
                    last.then_inc(xn_ready, 1)

            pipeline(dve, step)

            def hidden(n, v):
                dve.wait_ge(gelu_done, n + 1)
                dve.wait_ge(up_ready, n + 1)
                if not (isinstance(n, int) and n < 2):
                    dve.wait_ge(inter_low, n - 1)
                nc.vector.scalar_tensor_tensor(out=inter[:, v, :], in0=bU[v][:, :], scalar=1.0 / WS, in1=gel[:, v],
                                               op0=ALU.mult, op1=ALU.mult).then_inc(inter_ready, 1)
                dve.wait_ge(inter_high, n + 1)
                nc.vector.tensor_tensor(inter16[:, v, 1, :], inter[:, v, :], inter16[:, v, 0, :], ALU.subtract)\
                    .then_inc(inter_low, 1)

            def finish(k, u, stores):
                dve.wait_ge(down_done, (k + 1) * NTILES)
                dve.wait_ge(xres_ready, k + 1)
                if stores is not None:
                    dve.wait_ge(out_done[u], stores)
                for a in range(2):
                    nc.vector.scalar_tensor_tensor(
                        out=res[:, u, 2 * a:2 * a + 2, :], in0=bOut[a][:, :].rearrange("p (s c) -> p s c", s=2),
                        scalar=1.0 / WS, in1=xres[:, u, 2 * a:2 * a + 2, :], op0=ALU.mult, op1=ALU.add)\
                        .then_inc(acc_taken, 1)

            def chunk(k, u, head, stores):
                if head:
                    hidden(0, 0)
                else:
                    hidden(k * NTILES, 0)
                    finish(k - 1, 1 - u, stores)
                for n in range(1, NTILES):
                    hidden(k * NTILES + n, n % 2)

            chunk(0, 0, True, None)
            chunk(1, 1, False, None)
            chunk(2, 0, False, None)
            with dve.Fori(0, (NTOK // CH - 4) // 2) as j:
                for u in range(2):
                    chunk(j * 2 + (3 + u), 1 - u, False, (j + 1) * 16)
            chunk(NTOK // CH - 1, 1, False, (NTOK // CH // 2 - 1) * 16)
            finish(NTOK // CH - 1, 1, (NTOK // CH // 2 - 1) * 16)

        @block.tensor
        def _(pe):
            mm = nc.tensor.matmul

            def three(dst, lhs, rhs, start, stop):
                terms = [(a, pl, pr) for a in range(2) for pl, pr in ((0, 0), (0, 1), (1, 0))]
                for n, (a, pl, pr) in enumerate(terms):
                    last = mm(dst, lhs(a, pl), rhs(a, pr), start=start and n == 0,
                              stop=stop and n == len(terms) - 1, skip_group_check=True)
                return last

            def transpose_x(i):
                b = i + 2
                pe.wait_ge(x_high, b + 1)
                pe.wait_ge(x_low, b + 1)
                if not early(i, -2, 0):
                    pe.wait_ge(shT_kept, i - 1)
                if not early(i, 2, 1):
                    pe.wait_ge(xT_kept, b)
                for tt in range(2):
                    for a in range(2):
                        for part in range(2):
                            col = (2 * a + part) * T + tt * P
                            last = nc.tensor.transpose(bX16[:, col:col + P], x16[:, tt, part, a:C:2], idh[:, :])
                last.then_inc(xT_ready, 1)

            def project_qk(i, pair):
                b = i + 1
                if pair == 0:
                    pe.wait_ge(xT_kept, b + 1)
                    if not early(i, 1, 2):
                        pe.wait_ge(v_kept, i)
                    elif not early(i, 1, 1):
                        pe.wait_ge(rope_done, 2)
                else:
                    pe.wait_ge(rope_done, b * 2 + 1)
                tok = bass.ds(b * T, T)
                for n in range(2):
                    f = 2 * pair + n
                    last = three(bP[:, n * T:(n + 1) * T], lambda a, s: wqkv[:, a, s, f * P:(f + 1) * P],
                                 lambda a, s: xT[:, a, s, tok], n == 0, True)
                last.then_inc(proj_ready, 1)

            def project_v(i, proj_live):
                if proj_live:
                    pe.wait_ge(rope_done, (i + 2) * 2)
                else:
                    pe.wait_ge(v_kept, i)
                for kt in range(2):
                    last = three(bP[:, kt * C:(kt + 1) * C], lambda a, s: xT[:, a, s, bass.ds(i * T + kt * P, P)],
                                 lambda a, s: wqkv[:, a, s, 2 * C:3 * C], kt == 0, True)
                last.then_inc(v_ready, 1)

            def transpose_shift(i):
                pe.wait_ge(shift_split, i * 2)
                if isinstance(i, int):
                    pe.wait_ge(xT_kept, min(i + 3, B))
                else:
                    pe.wait_ge(xT_kept, i + 3)
                for qt in range(2):
                    last = nc.tensor.transpose(bX16[0:2 * H, qt * P:(qt + 1) * P],
                                               sh16[:, qt, :, :].rearrange("p s h -> p (s h)"), idh[:, :])
                last.then_inc(shT_ready, 1)

            def free_bank(taken, n0, k):
                if not (isinstance(n0, int) and n0 + k < 2):
                    pe.wait_ge(taken, n0 + (k - 1))

            def scores(i, u, g):
                if g % 2 == 0:
                    hf = g // 2
                    pe.wait_ge(stack_in[u][hf], i * 24 + (48 - 24 * u))
                    if not early(i, 0, 2):
                        pe.wait_ge(rows_zeroed, (i - 2) * 2 + hf + 1)
                    elif g == 0:
                        pe.wait_ge(filled, 7)
                        pe.wait_ge(queries_zero, 1)
                n0 = i * (GROUPS * FILLS)
                for f in range(FILLS):
                    free_bank(max_taken, n0, g * FILLS + f)
                    dst = bA[(g * FILLS + f) % 2]
                    for n in range(HEADS if f == 0 else 2):
                        h = HEADS * g + (n if f == 0 else 2 * (f - 1) + n)
                        w = P if f == 0 else T
                        last = mm(dst[:, n * w:(n + 1) * w], qs[:, u, h, T - P if f else 0:T if f else P],
                                  ks[:, u, h, 0:w], start=True, stop=True)
                    last.then_inc(scores_ready, 1)

            def shifted(i, u, g):
                v = 1 - u
                if g == 0:
                    pe.wait_ge(shift_in, i * 32)
                n0 = (i - 1) * (GROUPS * FILLS)
                for f in range(FILLS):
                    free_bank(exp_done, n0, g * FILLS + f)
                    dst = bB[(g * FILLS + f) % 2]
                    if f < 2:
                        diag = dst[:, :].rearrange("p (h t) -> p h t", h=2)[:, :, 0:P]
                        mm(diag, idb[:, :], mask_k_sb[:, 0:2 * P], start=True, stop=False, skip_group_check=True)
                    else:
                        mm(dst[:, :], idb[:, :], mask_k_sb[:, :], start=True, stop=False, skip_group_check=True)
                    for n in range(2 if f < 2 else HEADS):
                        h = HEADS * g + (2 * f + n if f < 2 else n)
                        w = T if f < 2 else P
                        kt = 0 if f < 2 else 1
                        last = mm(dst[:, n * w:(n + 1) * w], ks[:, v, h, kt * P:(kt + 1) * P], qs[:, v, h, T - w:T],
                                  start=False, stop=True, skip_group_check=True)
                    last.then_inc(shifted_ready, 1)

            def values(i, u, g):
                b = i - 1
                v = 1 - u
                pe.wait_ge(exp_done, (b * GROUPS + g + 1) * FILLS)
                if g == 0:
                    pe.wait_ge(v_kept, i)
                if g % 2 == 0 and not (early(i, -1, 1) and g == 0):
                    pe.wait_ge(oT_kept, b * 2 + g // 2)
                c0 = (g % 2) * T
                for n in range(HEADS):
                    h = HEADS * g + n
                    rows = slice(32 * n, 32 * n + 32)
                    p0 = pT[:, g % 2, n // 2, (n % 2) * T:(n % 2 + 1) * T]
                    p1 = pT[:, g % 2, 2, n * P:(n + 1) * P]
                    mm(bPV[rows, c0:c0 + T], V[:, v, 0, h * HP:h * HP + 32], p0, start=True, stop=False,
                       skip_group_check=True)
                for n in range(HEADS):
                    h = HEADS * g + n
                    rows = slice(32 * n, 32 * n + 32)
                    p1 = pT[:, g % 2, 2, n * P:(n + 1) * P]
                    last = mm(bPV[rows, c0 + P:c0 + T], V[:, v, 1, h * HP:h * HP + 32], p1, start=False, stop=True,
                              skip_group_check=True)
                last.then_inc(pv_done, 1)

            def transpose_o(i, qt):
                b = i - 2
                if qt == 0:
                    pe.wait_ge(oT_kept, b * 2 + 2)
                    if not early(i, -2, 1):
                        pe.wait_ge(attT_kept, b)
                else:
                    pe.wait_ge(o_taken, b * 2 + 1)
                for g in range(GROUPS):
                    c0 = (g % 2) * T + qt * P
                    last = nc.tensor.transpose(bO[:, g * P:(g + 1) * P], oT[:, g // 2, c0:c0 + P], idf[:, :])
                last.then_inc(o_ready, 1)

            def transpose_att(i):
                b = i - 2
                pe.wait_ge(att_high, b * 2 + 2)
                pe.wait_ge(att_low, b * 2 + 2)
                for qt in range(2):
                    for a in range(2):
                        for part in range(2):
                            col = (2 * a + part) * T + qt * P
                            last = nc.tensor.transpose(bO16[:, col:col + P], att16[:, qt, part, a * P:(a + 1) * P],
                                                       idh[:, :])
                last.then_inc(attT_ready, 1)

            def step(i, u, live):
                if live(2):
                    transpose_x(i)
                if live(1):
                    project_qk(i, 0)
                if live(-1):
                    transpose_shift(i)
                if live(0):
                    scores(i, u, 0)
                if live(1):
                    project_qk(i, 1)
                if live(0):
                    project_v(i, live(1))
                if live(-1):
                    shifted(i, u, 0)
                if live(0):
                    scores(i, u, 1)
                if live(-1):
                    shifted(i, u, 1)
                if live(-2):
                    transpose_o(i, 0)
                if live(-1):
                    values(i, u, 0)
                if live(0):
                    scores(i, u, 2)
                if live(-1):
                    shifted(i, u, 2)
                if live(-2):
                    transpose_o(i, 1)
                if live(-1):
                    values(i, u, 1)
                if live(0):
                    scores(i, u, 3)
                if live(-1):
                    shifted(i, u, 3)
                    values(i, u, 2)
                if live(-2):
                    transpose_att(i)
                if live(-1):
                    values(i, u, 3)

            pe.wait_ge(w_low, 3)
            pipeline(pe, step)

            def tile_cols(kind, n):
                return slice(kind * HID + n * P, kind * HID + (n + 1) * P)

            def gate_up(k, n):
                t0 = k * NTILES + n
                tok = bass.ds(k * CH, CH)
                v = n % 2
                if not (isinstance(k, int) and t0 < 2):
                    pe.wait_ge(gelu_done, t0 - 1)
                three(bG[v][:, :], lambda a, s: W[:, a, s, tile_cols(0, n)], lambda a, s: xT[:, a, s, tok], True, True)\
                    .then_inc(gate_ready, 1)
                if not (isinstance(k, int) and t0 < 2):
                    pe.wait_ge(inter_ready, t0 - 1)
                three(bU[v][:, :], lambda a, s: W[:, a, s, tile_cols(1, n)], lambda a, s: xT[:, a, s, tok], True, True)\
                    .then_inc(up_ready, 1)

            def project_out(k):
                if not (isinstance(k, int) and k == 0):
                    pe.wait_ge(acc_taken, k * 2)
                for s4 in range(SUB):
                    dst = bOut[s4 // 2][:, (s4 % 2) * C:(s4 % 2 + 1) * C]
                    three(dst, lambda a, s: attT[:, a, s, bass.ds(k * CH + s4 * P, P)], lambda a, s: wo[:, a, s, :],
                          s4 % 2 == 0, False)

            def down(k, n):
                t0 = k * NTILES + n
                v = n % 2
                pe.wait_ge(inter_high, t0 + 1)
                pe.wait_ge(inter_low, t0 + 1)
                j, par = n // 2, n % 2
                cols = slice(2 * HID + j * C, 2 * HID + (j + 1) * C)
                for s4 in range(SUB):
                    dst = bOut[s4 // 2][:, (s4 % 2) * C:(s4 % 2 + 1) * C]
                    for pl, pr in ((0, 0), (0, 1), (1, 0)):
                        last = mm(dst, inter16[:, v, pl, s4 * P:(s4 + 1) * P], W[:, par, pr, cols],
                                  start=False, stop=n == NTILES - 1, skip_group_check=True)
                last.then_inc(down_done, 1)
                return last

            pe.wait_ge(wf_low, SLICES)
            pe.wait_ge(wf_high, SLICES)
            pe.wait_ge(attT_kept, B)
            pe.wait_ge(max_taken, B * GROUPS * FILLS)
            pe.wait_ge(exp_done, B * GROUPS * FILLS)
            pe.wait_ge(v_kept, B)
            pe.wait_ge(shT_kept, B)

            def chunk(k, head):
                gate_up(k, 0)
                if not head:
                    down(k - 1, NTILES - 1)
                gate_up(k, 1)
                project_out(k)
                for n in range(2, NTILES):
                    down(k, n - 2)
                    gate_up(k, n)
                down(k, NTILES - 2)

            chunk(0, True)
            with pe.Fori(0, NTOK // CH - 1) as j:
                chunk(j + 1, False)
            down(NTOK // CH - 1, NTILES - 1)


def kernel(L0_attn_x, L0_attn_qkv_w, L0_attn_qkv_b, L0_attn_out_w, L0_attn_out_b, L0_ffn_gate_W_packed,
           L0_ffn_gate_scales, L0_ffn_up_W_packed, L0_ffn_up_scales, L0_ffn_down_W_packed, L0_ffn_down_scales):
    import concourse.bacc as bacc
    import ml_dtypes
    from concourse.bass_utils import run_bass_kernel_spmd

    a = np.asarray

    def even_odd_rows(w):
        return a(w).T.reshape(P, 2, -1)

    def hidden_order(w):
        return a(w).reshape(HID // (2 * P), P, 2, -1).transpose(3, 0, 2, 1).reshape(-1, HID)

    def down_order(w, p):
        return a(w).reshape(C, -1, p).transpose(2, 1, 0).reshape(p, -1)

    t = np.arange(T, dtype=np.float32)[:, None]
    angle = (t * (np.arange(0, D, 2, dtype=np.float32) / np.float32(D))[None, :]).astype(np.float64)
    emb = np.concatenate([np.sin(angle), np.cos(angle)], axis=-1).astype(np.float32)
    q, k = np.arange(P)[:, None], np.arange(P)[None, :]
    tri = np.where(k > q, np.float32(NEG), np.float32(0))
    arrays = {
        "x": a(L0_attn_x).reshape(NTOK // P, P, C),
        "qkv_wT": even_odd_rows(L0_attn_qkv_w),
        "qkv_b": a(L0_attn_qkv_b)[:2 * C].reshape(4, P).T,
        "v_b": a(L0_attn_qkv_b)[2 * C:],
        "out_wT": a(L0_attn_out_w).T.reshape(2, P, C).transpose(1, 0, 2),
        "out_b": a(L0_attn_out_b),
        "codes": np.concatenate([hidden_order(L0_ffn_gate_W_packed), hidden_order(L0_ffn_up_W_packed),
                                 down_order(L0_ffn_down_W_packed, P)], axis=1),
        "scales": np.concatenate([hidden_order(L0_ffn_gate_scales), hidden_order(L0_ffn_up_scales),
                                  down_order(L0_ffn_down_scales, P // 16)], axis=1),
        "emb": np.tile(emb.T / np.float32(WS), (P // D, 1)),
        "mask_q": np.concatenate([np.zeros((P, P), np.float32), tri], axis=1),
        "mask_k": np.tile(tri.T, (1, 4)).astype(ml_dtypes.bfloat16),
        "id_f32": np.eye(P, dtype=np.float32),
        "id_f16": np.eye(P, dtype=np.float16),
        "id_bf16": np.eye(P, dtype=ml_dtypes.bfloat16),
    }
    arrays = {f"in_{n}": np.ascontiguousarray(v) for n, v in arrays.items()}
    nc = bacc.Bacc("TRN2", target_bir_lowering=False, num_devices=1)
    aps = [nc.dram_tensor(n, v.shape, mybir.dt.from_np(v.dtype), kind="ExternalInput").ap() for n, v in arrays.items()]
    out = nc.dram_tensor("out", (NTOK // P, P, C), F32, kind="ExternalOutput").ap()
    build(nc, *aps, out)
    r = run_bass_kernel_spmd(nc, [arrays], core_ids=[0])
    return r.results[0]["out"].reshape(B, T, C)
```

```python
from contextlib import ExitStack

import numpy as np

import concourse.bass as bass
from concourse import mybir

F32 = mybir.dt.float32
F16 = mybir.dt.float16
BF16 = mybir.dt.bfloat16
I32 = mybir.dt.int32
ALU = mybir.AluOpType
ACT = mybir.ActivationFunctionType

P = 128
B, T, C, H = 16, 256, 256, 16
D = C // H
NTOK = B * T
HID = 2048
BLOCK = 32
EPS = 1e-5
WS = 16.0
CODE = 2.0 ** 14
NEG = -1e30
TWO_ONES = float(np.ones(2, np.float16).view(np.float32)[0])
HP = 20
VW = (H - 1) * HP + 32
HEADS = 4
GROUPS = H // HEADS
FILLS = 3
SLICES = 16
NW = 3 * HID
SW = NW // SLICES
CH = 512
SUB = CH // P
NTILES = HID // P


def build(nc, x, qkv_wT, qkv_b, v_b, out_wT, out_b, codes, scales, emb, mask_q, mask_k, id_f32, id_f16, id_bf16, out):
    ctx = ExitStack()
    with ctx:
        def sb(name, shape, dt):
            return ctx.enter_context(nc.sbuf_tensor(name, shape, dt))

        def sem(name):
            return ctx.enter_context(nc.semaphore(name))

        xT = sb("xT", [P, 2, 2, NTOK], F16)
        attT = sb("attT", [P, 2, 2, NTOK], F16)
        W = sb("W", [P, 2, 2, NW], F16)
        wqkv = sb("wqkv", [P, 2, 2, 3 * C], F16)
        wo = sb("wo", [P, 2, 2, C], F16)
        qs = sb("qs", [P, 2, H, T], F16)
        ks = sb("ks", [P, 2, H, T], F16)
        pT = sb("pT", [P, 2, FILLS, 512], F32)
        V = sb("V", [P, 2, 2, VW], F32)
        qk = sb("qk", [P, 4, T], F32)
        qk16 = sb("qk16", [P, 4, 2, T], F16)
        xs = sb("xs", [P, 2, C], F32)
        xn = sb("xn", [P, 2, C], F32)
        x16 = sb("x16", [P, 2, 2, C], F16)
        oT = sb("oT", [P, 2, 512], F32)
        att = sb("att", [P, 2, C], F32)
        att16 = sb("att16", [P, 2, 2, C], F16)
        emb_sb = sb("emb_sb", [P, T], F32)
        mask_q_sb = sb("mask_q_sb", [P, T], F32)
        mask_k_sb = sb("mask_k_sb", [P, 512], BF16)
        idf = sb("idf", [P, P], F32)
        idh = sb("idh", [P, P], F16)
        idb = sb("idb", [P, P], BF16)
        vb = sb("vb", [P, C], F32)
        qb = sb("qb", [P, 4], F32)
        qb16 = sb("qb16", [P, 4], F32)
        stats = sb("stats", [P, 2, 6], F32)
        moments = sb("moments", [P, 2, 2], F32)
        vareps = sb("vareps", [P, 2], F32)
        rstd = sb("rstd", [P, 2], F32)
        half = sb("half", [P, 2], F32)
        mx = sb("mx", [P, 2, H], F32)
        sh16 = sb("sh16", [P, 2, 2, H], F16)
        shT = sb("shT", [2 * H, T], F16)
        rden = sb("rden", [P, 2, H], F32)
        code = sb("code", [P, SW], I32)
        scale = sb("scale", [P, SW], F32)
        sign = sb("sign", [P, 2, SW], I32)
        wbits = sb("wbits", [P, 2, SW], I32)

        wstage = pT[:, :, :, :].rearrange("p a b c -> p (a b c)")
        wqkv_in = wstage[:, 0:6 * C].rearrange("p (a n) -> p a n", a=2)
        wo_in = wstage[:, 6 * C:8 * C].rearrange("p (a n) -> p a n", a=2)
        qs_f = qs[:, :, :, :].rearrange("p a h t -> p (a h t)")
        ks_f = ks[:, :, :, :].rearrange("p a h t -> p (a h t)").bitcast(F32)
        gel = qs_f[:, 0:2048].bitcast(F32).rearrange("p (b n) -> p b n", b=2)
        inter = qs_f[:, 2048:4096].bitcast(F32).rearrange("p (b n) -> p b n", b=2)
        inter16 = qs_f[:, 4096:6144].rearrange("p (b s n) -> p b s n", b=2, s=2)
        ob = qs_f[:, 6144:6144 + 2 * C].bitcast(F32)
        xres = ks_f[:, 0:2048].rearrange("p (b s c) -> p b s c", b=2, s=SUB)
        res = ks_f[:, 2048:4096].rearrange("p (b s c) -> p b s c", b=2, s=SUB)

        bank = [ctx.enter_context(nc.psum_tensor(f"bank{n}", [P, 512], F32)) for n in range(8)]
        bX, bO, bP, bPV = bank[0], bank[1], bank[2], bank[3]
        bA, bB = bank[4:6], bank[6:8]
        bX16 = bX[:, :].bitcast(F16)
        bO16 = bO[:, :].bitcast(F16)
        bG, bU, bOut = bA, bB, [bX, bP]

        stack = nc.dram_tensor("stack", [2, 2, 2, D, H, T], F16).ap()

        const_in, wts_in, x_in, codes_in = sem("const_in"), sem("wts_in"), sem("x_in"), sem("codes_in")
        stack_out = sem("stack_out")
        stack_in = [[sem(f"stack_in{v}{hf}") for hf in range(2)] for v in range(2)]
        shift_in, ob_in = sem("shift_in"), sem("ob_in")
        xres_in = [sem("xres_in0"), sem("xres_in1")]
        out_done = [sem("out_done0"), sem("out_done1")]
        filled, half_ready, v_zero, w_high, w_low = (
            sem("filled"), sem("half_ready"), sem("v_zero"), sem("w_high"), sem("w_low"))
        stats_done, moments_ready, eps_added, rstd_ready = (
            sem("stats_done"), sem("moments_ready"), sem("eps_added"), sem("rstd_ready"))
        xn_ready, x_high, x_low, xT_ready, xT_kept = (
            sem("xn_ready"), sem("x_high"), sem("x_low"), sem("xT_ready"), sem("xT_kept"))
        proj_ready, rope_done, qk_high, qk_low = sem("proj_ready"), sem("rope_done"), sem("qk_high"), sem("qk_low")
        v_ready, v_kept = sem("v_ready"), sem("v_kept")
        scores_ready, max_taken, shift_split = sem("scores_ready"), sem("max_taken"), sem("shift_split")
        shT_ready, shT_kept, rows_zeroed = sem("shT_ready"), sem("shT_kept"), sem("rows_zeroed")
        shifted_ready, exp_done, pv_done, oT_kept = (
            sem("shifted_ready"), sem("exp_done"), sem("pv_done"), sem("oT_kept"))
        o_ready, rden_ready, o_taken, att_high, att_low = (
            sem("o_ready"), sem("rden_ready"), sem("o_taken"), sem("att_high"), sem("att_low"))
        attT_ready, attT_kept = sem("attT_ready"), sem("attT_kept")
        bits_step, bits_ready, scale_ready, wf_ready, wf_high, wf_low = (
            sem("bits_step"), sem("bits_ready"), sem("scale_ready"), sem("wf_ready"), sem("wf_high"), sem("wf_low"))
        gate_ready, up_ready, gelu_done, inter_ready, inter_high, inter_low = (
            sem("gate_ready"), sem("up_ready"), sem("gelu_done"), sem("inter_ready"), sem("inter_high"), sem("inter_low"))
        down_done, acc_taken, xres_ready = (
            sem("down_done"), sem("acc_taken"), sem("xres_ready"))

        block = ctx.enter_context(nc.Block())

        FIRST, LOOP, LAST = -4, (3, 11), B + 2

        def pipeline(eng, step):
            def fixed(i):
                step(i, i % 2, lambda lag: 0 <= i + lag < B)
            for i in range(FIRST, LOOP[0]):
                fixed(i)
            with eng.Fori(0, (LOOP[1] - LOOP[0]) // 2) as j:
                for u in (0, 1):
                    step(j * 2 + (LOOP[0] + u), (LOOP[0] + u) % 2, lambda lag: True)
            for i in range(LOOP[1], LAST):
                fixed(i)

        def wait_apart(eng, semaphore, value):
            if not isinstance(value, int):
                value = eng.to_reg(value)
                eng.wait_ge(semaphore, 1)
            eng.wait_ge(semaphore, value)

        def early(i, lag, n):
            return isinstance(i, int) and i + lag < n

        @block.sync
        def _(sp):
            def load_x(b):
                sp.dma_start(xs[:, :, :], x[bass.ds(b * 2, 2)].rearrange("a p c -> p a c")).then_inc(x_in, 16)

            load_x(0)
            for dst, src in ((idh, id_f16), (qb, qkv_b), (emb_sb, emb), (mask_q_sb, mask_q), (mask_k_sb, mask_k),
                             (idf, id_f32), (idb, id_bf16)):
                sp.dma_start(dst[:, :], src).then_inc(const_in, 16)
            sp.dma_start(vb[:, :], v_b.partition_broadcast(P)).then_inc(const_in, 16)

            def load_stack(i, u, hf):
                v = 1 - u
                if not early(i, 1, 2):
                    sp.wait_ge(shifted_ready, (i - 1) * (GROUPS * FILLS) + 6 * (hf + 1))
                hs = slice(8 * hf, 8 * hf + 8)
                q0 = stack[v, 0, :, :, hs, :]
                k0 = stack[v, 1, :, :, hs, :]
                n = 8 * T
                src = bass.AP(q0.tensor, q0.offset, [[0, 2], [H * T, 2 * D], [1, n]])
                sp.dma_start(qs[0:4 * D, v, hs, :].rearrange("p h t -> p (h t)"), src).then_inc(stack_in[v][hf], 16)
                for part in range(2):
                    src = bass.AP(k0.tensor, k0.offset + part * D * H * T, [[0, 2], [H * T, D], [1, n]])
                    dst = ks[2 * part * D:2 * (part + 1) * D, v, hs, :].rearrange("p h t -> p (h t)")
                    sp.dma_start(dst, src).then_inc(stack_in[v][hf], 16)

            def step(i, u, live):
                if live(-1):
                    sp.wait_ge(shT_kept, i)
                    for part in range(2):
                        r = 4 * D + part
                        sp.dma_start(qs[r:r + 1, 1 - u, :, :], shT[part * H:(part + 1) * H, :]).then_inc(shift_in, 16)
                if live(4) and not early(i, 4, 1):
                    sp.wait_ge(xn_ready, i + 4)
                    load_x(i + 4)
                if live(0):
                    if not early(i, 0, 1):
                        sp.wait_ge(bits_ready, i)
                        sp.wait_ge(wf_ready, i)
                    sp.dma_start(code[:, :], codes[:, bass.ds(i * SW, SW)]).then_inc(codes_in, 16)
                    s0 = scales[:, bass.ds(i * SW, SW)]
                    src = bass.AP(s0.tensor, s0.offset, [[NW, P // 16], [0, 16], [1, SW]])
                    sp.dma_start(scale[:, :], src).then_inc(codes_in, 16)
                if live(1):
                    sp.wait_ge(stack_out, (i + 2) * 128)
                    load_stack(i, u, 0)
                if live(2):
                    b = i + 2
                    sp.wait_ge(qk_high, b + 1)
                    sp.wait_ge(qk_low, b + 1)
                    if not early(i, 2, 2):
                        for hf in range(2):
                            sp.wait_ge(stack_in[u][hf], i * 24 + (48 - 24 * u))
                    for f in range(4):
                        for part in range(2):
                            h0 = 8 * (f % 2)
                            dst = stack[u, f // 2, part].rearrange("d h t -> h d t")[h0:h0 + 8]
                            sp.dma_start(dst, qk16[:, f, part, :]).then_inc(stack_out, 16)
                if live(1):
                    load_stack(i, u, 1)

            pipeline(sp, step)

            sp.wait_ge(pv_done, B * GROUPS)
            sp.dma_start(ob, out_b.partition_broadcast(P)).then_inc(ob_in, 16)
            xc = x.rearrange("(k s) p c -> k p s c", s=SUB)
            oc = out.rearrange("(k s) p c -> k p s c", s=SUB)
            for k in range(2):
                sp.dma_start(xres[:, k], xc[k]).then_inc(xres_in[k], 16)

            def store(k, u):
                sp.wait_ge(acc_taken, (k + 1) * 2)
                sp.dma_start(oc[k] if isinstance(k, int) else oc[bass.ds(k, 1)].rearrange("k p s c -> p (k s) c"),
                             res[:, u]).then_inc(out_done[u], 16)

            with sp.Fori(0, NTOK // CH // 2 - 1) as j:
                for u in range(2):
                    store(j * 2 + u, u)
                    sp.dma_start(xres[:, u], xc[bass.ds(j * 2 + (2 + u), 1)].rearrange("k p s c -> p (k s) c"))\
                      .then_inc(xres_in[u], 16)
            for u in range(2):
                store(NTOK // CH - 2 + u, u)
            for u in range(2):
                sp.wait_ge(out_done[u], NTOK // CH // 2 * 16)

        @block.gpsimd
        def _(pool):
            nc.gpsimd.memset(half[:, :], -0.5).then_inc(half_ready, 1)
            pool.wait_ge(half_ready, 1)
            nc.gpsimd.memset(V[:, :, :, :], 0.0).then_inc(v_zero, 1)

            def zero_rows(i, u, hf, before):
                pool.wait_ge(*before)
                wait_apart(pool, shifted_ready, (i - 1) * (GROUPS * FILLS) + 6 * (hf + 1))
                nc.gpsimd.memset(qs[64:66, 1 - u, 8 * hf:8 * hf + 8, :].bitcast(F32), 0.0).then_inc(rows_zeroed, 1)
                pool.wait_ge(rows_zeroed, (i - 1) * 2 + hf + 1)

            def step(i, u, live):
                if live(-1):
                    wait_apart(pool, codes_in, i * 32)
                    nc.gpsimd.tensor_scalar(scale[:, :], scale[:, :], CODE * WS, None, ALU.mult).then_inc(scale_ready, 1)
                    pool.wait_ge(scale_ready, i)
                    pool.wait_ge(bits_ready, i)
                    val = wbits[:, :, :].bitcast(F16).rearrange("p a (n e) -> p a n e", e=2)[:, :, :, 0]
                    sc = scale[:, :].unsqueeze(1).broadcast_to([P, 2, SW])
                    nc.gpsimd.tensor_tensor(wbits[:, :, :].bitcast(F32), val, sc, ALU.mult).then_inc(wf_ready, 1)
                if live(2):
                    b = i + 2
                    pool.wait_ge(qk_high, b + 1)
                    if not early(i, 2, 1):
                        pool.wait_ge(stack_out, b * 128)
                    nc.gpsimd.tensor_tensor(qk16[:, :, 1, :], qk[:, :, :], qk16[:, :, 0, :], ALU.subtract)\
                        .then_inc(qk_low, 1)
                if live(1) and not early(i, 1, 2):
                    zero_rows(i, u, 0, (qk_low, i + 3) if live(2) else (wf_ready, i))
                if live(-2):
                    for qt in range(2):
                        pool.wait_ge(att_high, (i - 2) * 2 + qt + 1)
                        nc.gpsimd.tensor_tensor(att16[:, qt, 1, :], att[:, qt, :], att16[:, qt, 0, :], ALU.subtract)\
                            .then_inc(att_low, 1)
                if live(-1):
                    pool.wait_ge(wf_high, i)
                    o = bass.ds((i - 1) * SW, SW)
                    nc.gpsimd.tensor_tensor(W[:, :, 1, o], wbits[:, :, :].bitcast(F32), W[:, :, 0, o], ALU.subtract)\
                        .then_inc(wf_low, 1)
                if live(4):
                    b = i + 4
                    wait_apart(pool, moments_ready, b + 1)
                    nc.gpsimd.tensor_scalar(vareps[:, :], moments[:, :, 1], EPS, None, ALU.add).then_inc(eps_added, 1)
                    pool.wait_ge(eps_added, b + 1)
                    if early(i, 4, 1):
                        pool.wait_ge(half_ready, 1)
                    else:
                        pool.wait_ge(xn_ready, b)
                    nc.gpsimd.tensor_tensor(rstd[:, :], vareps[:, :], half[:, :], ALU.pow).then_inc(rstd_ready, 1)
                    pool.wait_ge(x_high, b + 1)
                    nc.gpsimd.tensor_tensor(x16[:, :, 1, :], xn[:, :, :], x16[:, :, 0, :], ALU.subtract)\
                        .then_inc(x_low, 1)
                if live(1) and not early(i, 1, 2):
                    zero_rows(i, u, 1, (x_low, i + 5) if live(4) else (wf_low, i))

            pipeline(pool, step)

            pool.wait_ge(ob_in, 16)

            def residual(k, u):
                pool.wait_ge(xres_in[u], (k // 2 + 1) * 16 if isinstance(k, int) else (k + 1) * 16)
                nc.gpsimd.tensor_tensor(xres[:, u], xres[:, u], ob.unsqueeze(1).broadcast_to([P, SUB, C]), ALU.add)\
                    .then_inc(xres_ready, 1)

            with pool.Fori(0, NTOK // CH // 2) as j:
                for u in range(2):
                    residual(j + 0, u)

        @block.scalar
        def _(act):
            act.dma_start(wqkv_in, qkv_wT).then_inc(wts_in, 16)
            act.dma_start(wo_in, out_wT).then_inc(wts_in, 16)
            act.wait_ge(wts_in, 32)
            nc.scalar.activation(wqkv[:, :, 0, :], wqkv_in, ACT.Copy, scale=WS).then_inc(w_high, 1)
            nc.scalar.activation(wo[:, :, 0, :], wo_in, ACT.Copy, scale=WS).then_inc(w_high, 1)

            def exps(i, first, last):
                b = i - 1
                for m in range(first, last):
                    g, f = m // FILLS, m % FILLS
                    if f == 0:
                        if g < 2 and early(i, -1, 1):
                            act.wait_ge(w_low, 2)
                        else:
                            act.wait_ge(pv_done, b * GROUPS + g - 1)
                    act.wait_ge(shifted_ready, b * (GROUPS * FILLS) + m + 1)
                    nc.scalar.activation(pT[:, g % 2, f, :], bB[m % 2][:, :], ACT.Exp, scale=D ** -0.5)\
                        .then_inc(exp_done, 1)

            def keep_o(i, hf):
                b = i - 1
                act.wait_ge(pv_done, b * GROUPS + 2 * hf + 2)
                if not early(i, -1, 1):
                    act.wait_ge(o_ready, b * 2)
                nc.scalar.activation(oT[:, hf, :], bPV[:, :], ACT.Copy).then_inc(oT_kept, 1)

            def att_hi(i, qt):
                b = i - 2
                act.wait_ge(o_taken, b * 2 + qt + 1)
                if not early(i, -2, 1):
                    act.wait_ge(attT_ready, b)
                nc.scalar.activation(att16[:, qt, 0, :], att[:, qt, :], ACT.Copy).then_inc(att_high, 1)

            def step(i, u, live):
                if live(3):
                    b = i + 3
                    act.wait_ge(xT_ready, b + 1)
                    nc.scalar.activation(xT[:, :, :, bass.ds(b * T, T)].rearrange("p a s t -> p (a s) t"),
                                         bX16.rearrange("p (a t) -> p a t", a=4), ACT.Copy).then_inc(xT_kept, 1)
                if live(-1):
                    exps(i, 0, 3)
                if live(2):
                    b = i + 2
                    act.wait_ge(rope_done, (b + 1) * 2)
                    if not early(i, 2, 1):
                        act.wait_ge(stack_out, b * 128)
                    nc.scalar.activation(qk16[:, :, 0, :], qk[:, :, :], ACT.Copy).then_inc(qk_high, 1)
                if live(-1):
                    exps(i, 3, 5)
                    act.wait_ge(wf_ready, i)
                    nc.scalar.activation(W[:, :, 0, bass.ds((i - 1) * SW, SW)], wbits[:, :, :].bitcast(F32), ACT.Copy)\
                        .then_inc(wf_high, 1)
                    exps(i, 5, 6)
                if live(-2):
                    att_hi(i, 0)
                if live(-1):
                    exps(i, 6, 8)
                    keep_o(i, 0)
                    exps(i, 8, 9)
                if live(-2):
                    att_hi(i, 1)
                if live(-1):
                    exps(i, 9, 10)
                if live(4):
                    b = i + 4
                    act.wait_ge(xn_ready, b + 1)
                    if not early(i, 4, 1):
                        act.wait_ge(xT_ready, b)
                    nc.scalar.activation(x16[:, :, 0, :], xn[:, :, :], ACT.Copy).then_inc(x_high, 1)
                if live(-1):
                    exps(i, 10, 12)
                if live(-2):
                    act.wait_ge(attT_ready, i - 1)
                    nc.scalar.activation(attT[:, :, :, bass.ds((i - 2) * T, T)].rearrange("p a s t -> p (a s) t"),
                                         bO16.rearrange("p (a t) -> p a t", a=4), ACT.Copy).then_inc(attT_kept, 1)
                if live(0):
                    act.wait_ge(shT_ready, i + 1)
                    if not early(i, 0, 1):
                        act.wait_ge(shift_in, i * 32)
                    nc.scalar.activation(shT[:, :], bX16[0:2 * H, 0:T], ACT.Copy).then_inc(shT_kept, 1)
                if live(-1):
                    keep_o(i, 1)

            pipeline(act, step)

            def mlp(n, v):
                act.wait_ge(gate_ready, n + 1)
                if not (isinstance(n, int) and n < 2):
                    act.wait_ge(inter_ready, n - 1)
                nc.scalar.activation(gel[:, v], bG[v][:, :], ACT.Gelu_apprx_tanh, scale=1.0 / WS).then_inc(gelu_done, 1)
                act.wait_ge(inter_ready, n + 1)
                if not (isinstance(n, int) and n < 2):
                    act.wait_ge(down_done, n - 1)
                nc.scalar.activation(inter16[:, v, 0, :], inter[:, v, :], ACT.Copy).then_inc(inter_high, 1)

            for n in range(2):
                mlp(n, n)
            with act.Fori(0, NTOK // CH * NTILES // 2 - 1) as j:
                for v in range(2):
                    mlp(j * 2 + (2 + v), v)

        @block.vector
        def _(dve):
            dve.wait_ge(w_high, 1)
            nc.vector.scalar_tensor_tensor(out=wqkv[:, :, 1, :], in0=wqkv_in, scalar=WS, in1=wqkv[:, :, 0, :],
                                           op0=ALU.mult, op1=ALU.subtract).then_inc(w_low, 1)
            dve.wait_ge(w_high, 2)
            nc.vector.scalar_tensor_tensor(out=wo[:, :, 1, :], in0=wo_in, scalar=WS, in1=wo[:, :, 0, :],
                                           op0=ALU.mult, op1=ALU.subtract).then_inc(w_low, 1)
            dve.wait_ge(const_in, 8 * 16)
            nc.vector.tensor_scalar(qb16[:, :], qb[:, :], WS, None, ALU.mult).then_inc(w_low, 1)
            dve.wait_ge(w_low, 3)

            def fill():
                nc.vector.memset(qs[64:128, :, :, :].bitcast(F32), 0.0).then_inc(filled, 1)
                nc.vector.memset(ks[64:128, :, :, :].bitcast(F32), 0.0).then_inc(filled, 1)
                dve.wait_ge(filled, 2)
                nc.vector.memset(ks[64:66, :, :, :].bitcast(F32), TWO_ONES).then_inc(filled, 1)
                dve.wait_ge(v_zero, 1)
                for a in range(2):
                    for kt in range(2):
                        nc.vector.memset(V[:, a, kt, D:D + (H - 1) * HP + 1:HP], 1.0).then_inc(filled, 1)

            def rope(i, pair):
                b = i + 2
                dve.wait_ge(proj_ready, b * 2 + pair + 1)
                if pair == 0 and not early(i, 2, 1):
                    dve.wait_ge(qk_low, b)
                for n in range(2):
                    f = 2 * pair + n
                    last = nc.vector.scalar_tensor_tensor(
                        out=qk[:, f, :], in0=bP[:, n * T:(n + 1) * T], scalar=qb16[:, f:f + 1], in1=emb_sb[:, :],
                        op0=ALU.add, op1=ALU.mult)
                last.then_inc(rope_done, 1)

            def row_max(i, first, last_fill):
                for m in range(first, last_fill):
                    g, f = m // FILLS, m % FILLS
                    wait_apart(dve, scores_ready, i * (GROUPS * FILLS) + m + 1)
                    s = bA[m % 2]
                    for n in range(HEADS if f == 0 else 2):
                        if f == 0:
                            h, qt, w = HEADS * g + n, 0, P
                        else:
                            h, qt, w = HEADS * g + 2 * (f - 1) + n, 1, T
                        last = nc.vector.tensor_tensor_reduce(
                            s[:, n * w:(n + 1) * w], s[:, n * w:(n + 1) * w], mask_q_sb[:, T - w:T], 1.0, -3e38,
                            ALU.add, ALU.max, mx[:, qt, h:h + 1])
                    last.then_inc(max_taken, 1)

            def normalise(i, qt):
                b = i - 2
                dve.wait_ge(o_ready, b * 2 + qt + 1)
                o = bO[:, :].rearrange("p (h e) -> p h e", e=32)
                nc.vector.reciprocal(rden[:, qt, :], o[:, :, D]).then_inc(rden_ready, 1)
                dve.wait_ge(rden_ready, b * 2 + qt + 1)
                if not early(i, -2, 1):
                    dve.wait_ge(att_low, (b - 1) * 2 + qt + 1)
                nc.vector.tensor_tensor(att[:, qt, :].rearrange("p (h d) -> p h d", d=D), o[:, :, 0:D],
                                        rden[:, qt, :].unsqueeze(2).broadcast_to([P, H, D]), ALU.mult)\
                    .then_inc(o_taken, 1)

            def step(i, u, live):
                if isinstance(i, int) and i == FIRST + 1:
                    fill()
                if live(0):
                    row_max(i, 0, 1)
                if live(2):
                    rope(i, 0)
                if live(0):
                    row_max(i, 1, 3)
                if live(2):
                    rope(i, 1)
                if live(0):
                    row_max(i, 3, 5)
                    dve.wait_ge(v_ready, i + 1)
                    if not early(i, 0, 2):
                        dve.wait_ge(pv_done, (i - 1) * GROUPS)
                    for kt in range(2):
                        dst = V[:, u, kt, 0:H * HP].rearrange("p (h e) -> p h e", e=HP)[:, :, 0:D]
                        last = nc.vector.scalar_tensor_tensor(
                            out=dst, in0=bP[:, kt * C:(kt + 1) * C].rearrange("p (h d) -> p h d", d=D),
                            scalar=1.0 / WS, in1=vb[:, :].rearrange("p (h d) -> p h d", d=D), op0=ALU.mult, op1=ALU.add)
                    last.then_inc(v_kept, 1)
                    row_max(i, 5, 6)
                if live(-2):
                    normalise(i, 0)
                if live(4):
                    b = i + 4
                    dve.wait_ge(x_in, (b + 1) * 16)
                    for tt in range(2):
                        last = nc.vector.bn_stats(stats[:, tt, :], xs[:, tt, :])
                    last.then_inc(stats_done, 1)
                if live(0):
                    row_max(i, 6, 7)
                if live(4):
                    wait_apart(dve, stats_done, i + 5)
                    for tt in range(2):
                        last = nc.vector.bn_aggr(moments[:, tt, :], stats[:, tt, :])
                    last.then_inc(moments_ready, 1)
                if live(0):
                    row_max(i, 7, 9)
                if live(-2):
                    normalise(i, 1)
                if live(4):
                    b = i + 4
                    dve.wait_ge(rstd_ready, b + 1)
                    if not early(i, 4, 1):
                        dve.wait_ge(x_low, b)
                    for tt in range(2):
                        last = nc.vector.tensor_scalar(xn[:, tt, :], xs[:, tt, :], moments[:, tt, 0:1],
                                                       rstd[:, tt:tt + 1], ALU.subtract, ALU.mult)
                    last.then_inc(xn_ready, 1)
                if live(0):
                    row_max(i, 9, 12)
                    dve.wait_ge(max_taken, (i + 1) * (GROUPS * FILLS))
                    if not early(i, 0, 1):
                        dve.wait_ge(shT_ready, i)
                    nc.vector.tensor_scalar(sh16[:, :, 0, :], mx[:, :, :], -1.0, None, ALU.mult).then_inc(shift_split, 1)
                    dve.wait_ge(shift_split, i * 2 + 1)
                    nc.vector.scalar_tensor_tensor(out=sh16[:, :, 1, :], in0=mx[:, :, :], scalar=-1.0,
                                                   in1=sh16[:, :, 0, :], op0=ALU.mult, op1=ALU.subtract)\
                        .then_inc(shift_split, 1)
                    dve.wait_ge(codes_in, (i + 1) * 32)
                    if not early(i, 0, 1):
                        dve.wait_ge(wf_low, i)
                    for par, (m, s) in enumerate(((0x7, 9), (0x70, 5))):
                        nc.vector.tensor_scalar(wbits[:, par, :], code[:, :], m, s, ALU.bitwise_and,
                                                ALU.logical_shift_left)
                        last = nc.vector.tensor_scalar(sign[:, par, :], code[:, :], (8, 128)[par], (12, 8)[par],
                                                       ALU.bitwise_and, ALU.logical_shift_left)
                    last.then_inc(bits_step, 1)
                    dve.wait_ge(bits_step, i + 1)
                    nc.vector.tensor_tensor(wbits[:, :, :], wbits[:, :, :], sign[:, :, :], ALU.bitwise_or)\
                        .then_inc(bits_ready, 1)

            pipeline(dve, step)

            def hidden(n, v):
                dve.wait_ge(gelu_done, n + 1)
                dve.wait_ge(up_ready, n + 1)
                if not (isinstance(n, int) and n < 2):
                    dve.wait_ge(inter_low, n - 1)
                nc.vector.scalar_tensor_tensor(out=inter[:, v, :], in0=bU[v][:, :], scalar=1.0 / WS, in1=gel[:, v],
                                               op0=ALU.mult, op1=ALU.mult).then_inc(inter_ready, 1)
                dve.wait_ge(inter_high, n + 1)
                nc.vector.tensor_tensor(inter16[:, v, 1, :], inter[:, v, :], inter16[:, v, 0, :], ALU.subtract)\
                    .then_inc(inter_low, 1)

            def finish(k, u, stores):
                dve.wait_ge(down_done, (k + 1) * NTILES)
                dve.wait_ge(xres_ready, k + 1)
                if stores is not None:
                    dve.wait_ge(out_done[u], stores)
                for a in range(2):
                    nc.vector.scalar_tensor_tensor(
                        out=res[:, u, 2 * a:2 * a + 2, :], in0=bOut[a][:, :].rearrange("p (s c) -> p s c", s=2),
                        scalar=1.0 / WS, in1=xres[:, u, 2 * a:2 * a + 2, :], op0=ALU.mult, op1=ALU.add)\
                        .then_inc(acc_taken, 1)

            def chunk(k, u, head, stores):
                if head:
                    hidden(0, 0)
                else:
                    hidden(k * NTILES, 0)
                    finish(k - 1, 1 - u, stores)
                for n in range(1, NTILES):
                    hidden(k * NTILES + n, n % 2)

            chunk(0, 0, True, None)
            chunk(1, 1, False, None)
            chunk(2, 0, False, None)
            with dve.Fori(0, (NTOK // CH - 4) // 2) as j:
                for u in range(2):
                    chunk(j * 2 + (3 + u), 1 - u, False, (j + 1) * 16)
            chunk(NTOK // CH - 1, 1, False, (NTOK // CH // 2 - 1) * 16)
            finish(NTOK // CH - 1, 1, (NTOK // CH // 2 - 1) * 16)

        @block.tensor
        def _(pe):
            mm = nc.tensor.matmul

            def three(dst, lhs, rhs, start, stop):
                terms = [(a, pl, pr) for a in range(2) for pl, pr in ((0, 0), (0, 1), (1, 0))]
                for n, (a, pl, pr) in enumerate(terms):
                    last = mm(dst, lhs(a, pl), rhs(a, pr), start=start and n == 0,
                              stop=stop and n == len(terms) - 1, skip_group_check=True)
                return last

            def transpose_x(i):
                b = i + 3
                pe.wait_ge(x_high, b + 1)
                pe.wait_ge(x_low, b + 1)
                if not early(i, -1, 0):
                    pe.wait_ge(shT_kept, i)
                if not early(i, 3, 1):
                    pe.wait_ge(xT_kept, b)
                for tt in range(2):
                    for a in range(2):
                        for part in range(2):
                            col = (2 * a + part) * T + tt * P
                            last = nc.tensor.transpose(bX16[:, col:col + P], x16[:, tt, part, a:C:2], idh[:, :])
                last.then_inc(xT_ready, 1)

            def project_qk(i, pair):
                b = i + 2
                if pair == 0:
                    pe.wait_ge(xT_kept, b + 1)
                    if not early(i, -1, 0):
                        pe.wait_ge(v_kept, i)
                    elif not early(i, 2, 1):
                        pe.wait_ge(rope_done, b * 2)
                else:
                    pe.wait_ge(rope_done, b * 2 + 1)
                tok = bass.ds(b * T, T)
                for n in range(2):
                    f = 2 * pair + n
                    last = three(bP[:, n * T:(n + 1) * T], lambda a, s: wqkv[:, a, s, f * P:(f + 1) * P],
                                 lambda a, s: xT[:, a, s, tok], n == 0, True)
                last.then_inc(proj_ready, 1)

            def project_v(i, proj_live):
                if proj_live:
                    pe.wait_ge(rope_done, (i + 3) * 2)
                else:
                    pe.wait_ge(v_kept, i)
                for kt in range(2):
                    last = three(bP[:, kt * C:(kt + 1) * C], lambda a, s: xT[:, a, s, bass.ds(i * T + kt * P, P)],
                                 lambda a, s: wqkv[:, a, s, 2 * C:3 * C], kt == 0, True)
                last.then_inc(v_ready, 1)

            def transpose_shift(i):
                pe.wait_ge(shift_split, i * 2 + 2)
                pe.wait_ge(xT_kept, min(i + 4, B) if isinstance(i, int) else i + 4)
                for qt in range(2):
                    last = nc.tensor.transpose(bX16[0:2 * H, qt * P:(qt + 1) * P],
                                               sh16[:, qt, :, :].rearrange("p s h -> p (s h)"), idh[:, :])
                last.then_inc(shT_ready, 1)

            def free_bank(taken, n0, k):
                if not (isinstance(n0, int) and n0 + k < 2):
                    pe.wait_ge(taken, n0 + (k - 1))

            def scores(i, u, m):
                g, f = m // FILLS, m % FILLS
                if m % 6 == 0:
                    hf = m // 6
                    pe.wait_ge(stack_in[u][hf], i * 24 + (48 - 24 * u))
                    if not early(i, 0, 2):
                        pe.wait_ge(rows_zeroed, (i - 2) * 2 + hf + 1)
                    elif m == 0:
                        pe.wait_ge(filled, 7)
                free_bank(max_taken, i * (GROUPS * FILLS), m)
                dst = bA[m % 2]
                for n in range(HEADS if f == 0 else 2):
                    h = HEADS * g + (n if f == 0 else 2 * (f - 1) + n)
                    w = P if f == 0 else T
                    last = mm(dst[:, n * w:(n + 1) * w], qs[:, u, h, T - P if f else 0:T if f else P],
                              ks[:, u, h, 0:w], start=True, stop=True)
                last.then_inc(scores_ready, 1)

            def shifted(i, u, m):
                g, f = m // FILLS, m % FILLS
                v = 1 - u
                if m == 0:
                    pe.wait_ge(shift_in, i * 32)
                free_bank(exp_done, (i - 1) * (GROUPS * FILLS), m)
                dst = bB[m % 2]
                if f < 2:
                    diag = dst[:, :].rearrange("p (h t) -> p h t", h=2)[:, :, 0:P]
                    mm(diag, idb[:, :], mask_k_sb[:, 0:2 * P], start=True, stop=False, skip_group_check=True)
                else:
                    mm(dst[:, :], idb[:, :], mask_k_sb[:, :], start=True, stop=False, skip_group_check=True)
                for n in range(2 if f < 2 else HEADS):
                    h = HEADS * g + (2 * f + n if f < 2 else n)
                    w = T if f < 2 else P
                    kt = 0 if f < 2 else 1
                    last = mm(dst[:, n * w:(n + 1) * w], ks[:, v, h, kt * P:(kt + 1) * P], qs[:, v, h, T - w:T],
                              start=False, stop=True, skip_group_check=True)
                last.then_inc(shifted_ready, 1)

            def values(i, u, g):
                b = i - 1
                v = 1 - u
                pe.wait_ge(exp_done, (b * GROUPS + g + 1) * FILLS)
                if g == 0:
                    pe.wait_ge(v_kept, i)
                if g % 2 == 0 and not (early(i, -1, 1) and g == 0):
                    pe.wait_ge(oT_kept, b * 2 + g // 2)
                c0 = (g % 2) * T
                for n in range(HEADS):
                    h = HEADS * g + n
                    rows = slice(32 * n, 32 * n + 32)
                    p0 = pT[:, g % 2, n // 2, (n % 2) * T:(n % 2 + 1) * T]
                    mm(bPV[rows, c0:c0 + T], V[:, v, 0, h * HP:h * HP + 32], p0, start=True, stop=False,
                       skip_group_check=True)
                for n in range(HEADS):
                    h = HEADS * g + n
                    rows = slice(32 * n, 32 * n + 32)
                    p1 = pT[:, g % 2, 2, n * P:(n + 1) * P]
                    last = mm(bPV[rows, c0 + P:c0 + T], V[:, v, 1, h * HP:h * HP + 32], p1, start=False, stop=True,
                              skip_group_check=True)
                last.then_inc(pv_done, 1)

            def transpose_o(i, qt):
                b = i - 2
                if qt == 0:
                    pe.wait_ge(oT_kept, b * 2 + 2)
                    if not early(i, -2, 1):
                        pe.wait_ge(attT_kept, b)
                else:
                    pe.wait_ge(o_taken, b * 2 + 1)
                for g in range(GROUPS):
                    c0 = (g % 2) * T + qt * P
                    last = nc.tensor.transpose(bO[:, g * P:(g + 1) * P], oT[:, g // 2, c0:c0 + P], idf[:, :])
                last.then_inc(o_ready, 1)

            def transpose_att(i):
                b = i - 2
                pe.wait_ge(att_high, b * 2 + 2)
                pe.wait_ge(att_low, b * 2 + 2)
                for qt in range(2):
                    for a in range(2):
                        for part in range(2):
                            col = (2 * a + part) * T + qt * P
                            last = nc.tensor.transpose(bO16[:, col:col + P], att16[:, qt, part, a * P:(a + 1) * P],
                                                       idh[:, :])
                last.then_inc(attT_ready, 1)

            def step(i, u, live):
                do = {"A": (0, scores), "S": (-1, shifted), "V": (-1, values)}

                def run(order):
                    for item in order.split():
                        lag, unit = do[item[0]]
                        if live(lag):
                            unit(i, u, int(item[1:]))

                if live(3):
                    transpose_x(i)
                run("A0")
                if live(2):
                    project_qk(i, 0)
                run("A1 S0 A2")
                if live(2):
                    project_qk(i, 1)
                run("S1 A3 S2 A4")
                if live(0):
                    project_v(i, live(2))
                run("S3 V0 A5 S4")
                if live(-2):
                    transpose_o(i, 0)
                run("A6 S5 A7 S6 V1 A8 S7")
                if live(-2):
                    transpose_o(i, 1)
                run("A9 S8 A10 S9 V2 A11 S10")
                if live(-2):
                    transpose_att(i)
                run("S11")
                if live(0):
                    transpose_shift(i)
                run("V3")

            pe.wait_ge(w_low, 3)
            pipeline(pe, step)

            def tile_cols(kind, n):
                return slice(kind * HID + n * P, kind * HID + (n + 1) * P)

            def gate_up(k, n):
                t0 = k * NTILES + n
                tok = bass.ds(k * CH, CH)
                v = n % 2
                if not (isinstance(k, int) and t0 < 2):
                    pe.wait_ge(gelu_done, t0 - 1)
                three(bG[v][:, :], lambda a, s: W[:, a, s, tile_cols(0, n)], lambda a, s: xT[:, a, s, tok], True, True)\
                    .then_inc(gate_ready, 1)
                if not (isinstance(k, int) and t0 < 2):
                    pe.wait_ge(inter_ready, t0 - 1)
                three(bU[v][:, :], lambda a, s: W[:, a, s, tile_cols(1, n)], lambda a, s: xT[:, a, s, tok], True, True)\
                    .then_inc(up_ready, 1)

            def project_out(k):
                if not (isinstance(k, int) and k == 0):
                    pe.wait_ge(acc_taken, k * 2)
                for s4 in range(SUB):
                    dst = bOut[s4 // 2][:, (s4 % 2) * C:(s4 % 2 + 1) * C]
                    three(dst, lambda a, s: attT[:, a, s, bass.ds(k * CH + s4 * P, P)], lambda a, s: wo[:, a, s, :],
                          s4 % 2 == 0, False)

            def down(k, n):
                t0 = k * NTILES + n
                v = n % 2
                pe.wait_ge(inter_high, t0 + 1)
                pe.wait_ge(inter_low, t0 + 1)
                j, par = n // 2, n % 2
                cols = slice(2 * HID + j * C, 2 * HID + (j + 1) * C)
                for s4 in range(SUB):
                    dst = bOut[s4 // 2][:, (s4 % 2) * C:(s4 % 2 + 1) * C]
                    for pl, pr in ((0, 0), (0, 1), (1, 0)):
                        last = mm(dst, inter16[:, v, pl, s4 * P:(s4 + 1) * P], W[:, par, pr, cols],
                                  start=False, stop=n == NTILES - 1, skip_group_check=True)
                last.then_inc(down_done, 1)
                return last

            pe.wait_ge(wf_low, SLICES)
            pe.wait_ge(wf_high, SLICES)
            pe.wait_ge(attT_kept, B)
            pe.wait_ge(max_taken, B * GROUPS * FILLS)
            pe.wait_ge(exp_done, B * GROUPS * FILLS)
            pe.wait_ge(v_kept, B)
            pe.wait_ge(shT_kept, B)

            def chunk(k, head):
                gate_up(k, 0)
                if not head:
                    down(k - 1, NTILES - 1)
                gate_up(k, 1)
                project_out(k)
                for n in range(2, NTILES):
                    down(k, n - 2)
                    gate_up(k, n)
                down(k, NTILES - 2)

            chunk(0, True)
            with pe.Fori(0, NTOK // CH - 1) as j:
                chunk(j + 1, False)
            down(NTOK // CH - 1, NTILES - 1)


def kernel(L0_attn_x, L0_attn_qkv_w, L0_attn_qkv_b, L0_attn_out_w, L0_attn_out_b, L0_ffn_gate_W_packed,
           L0_ffn_gate_scales, L0_ffn_up_W_packed, L0_ffn_up_scales, L0_ffn_down_W_packed, L0_ffn_down_scales):
    import concourse.bacc as bacc
    import ml_dtypes
    from concourse.bass_utils import run_bass_kernel_spmd

    a = np.asarray

    def even_odd_rows(w):
        return a(w).T.reshape(P, 2, -1)

    def hidden_order(w):
        return a(w).reshape(HID // (2 * P), P, 2, -1).transpose(3, 0, 2, 1).reshape(-1, HID)

    def down_order(w, p):
        return a(w).reshape(C, -1, p).transpose(2, 1, 0).reshape(p, -1)

    t = np.arange(T, dtype=np.float32)[:, None]
    angle = (t * (np.arange(0, D, 2, dtype=np.float32) / np.float32(D))[None, :]).astype(np.float64)
    emb = np.concatenate([np.sin(angle), np.cos(angle)], axis=-1).astype(np.float32)
    q, k = np.arange(P)[:, None], np.arange(P)[None, :]
    tri = np.where(k > q, np.float32(NEG), np.float32(0))
    arrays = {
        "x": a(L0_attn_x).reshape(NTOK // P, P, C),
        "qkv_wT": even_odd_rows(L0_attn_qkv_w),
        "qkv_b": a(L0_attn_qkv_b)[:2 * C].reshape(4, P).T,
        "v_b": a(L0_attn_qkv_b)[2 * C:],
        "out_wT": a(L0_attn_out_w).T.reshape(2, P, C).transpose(1, 0, 2),
        "out_b": a(L0_attn_out_b),
        "codes": np.concatenate([hidden_order(L0_ffn_gate_W_packed), hidden_order(L0_ffn_up_W_packed),
                                 down_order(L0_ffn_down_W_packed, P)], axis=1),
        "scales": np.concatenate([hidden_order(L0_ffn_gate_scales), hidden_order(L0_ffn_up_scales),
                                  down_order(L0_ffn_down_scales, P // 16)], axis=1),
        "emb": np.tile(emb.T / np.float32(WS), (P // D, 1)),
        "mask_q": np.concatenate([np.zeros((P, P), np.float32), tri], axis=1),
        "mask_k": np.tile(tri.T, (1, 4)).astype(ml_dtypes.bfloat16),
        "id_f32": np.eye(P, dtype=np.float32),
        "id_f16": np.eye(P, dtype=np.float16),
        "id_bf16": np.eye(P, dtype=ml_dtypes.bfloat16),
    }
    arrays = {f"in_{n}": np.ascontiguousarray(v) for n, v in arrays.items()}
    nc = bacc.Bacc("TRN2", target_bir_lowering=False, num_devices=1)
    aps = [nc.dram_tensor(n, v.shape, mybir.dt.from_np(v.dtype), kind="ExternalInput").ap() for n, v in arrays.items()]
    out = nc.dram_tensor("out", (NTOK // P, P, C), F32, kind="ExternalOutput").ap()
    build(nc, *aps, out)
    r = run_bass_kernel_spmd(nc, [arrays], core_ids=[0])
    return r.results[0]["out"].reshape(B, T, C)
```

```python
from contextlib import ExitStack

import numpy as np

import concourse.bass as bass
from concourse import mybir

F32 = mybir.dt.float32
F16 = mybir.dt.float16
BF16 = mybir.dt.bfloat16
I32 = mybir.dt.int32
ALU = mybir.AluOpType
ACT = mybir.ActivationFunctionType

P = 128
B, T, C, H = 16, 256, 256, 16
D = C // H
NTOK = B * T
HID = 2048
BLOCK = 32
EPS = 1e-5
WS = 16.0
CODE = 2.0 ** 14
NEG = -1e30
TWO_ONES = float(np.ones(2, np.float16).view(np.float32)[0])
HP = 20
VW = (H - 1) * HP + 32
HEADS = 4
GROUPS = H // HEADS
FILLS = 3
SLICES = 16
NW = 3 * HID
SW = NW // SLICES
CH = 512
SUB = CH // P
NTILES = HID // P


def build(nc, x, qkv_wT, qkv_b, v_b, out_wT, out_b, codes, scales, emb, mask_q, mask_k, id_f32, id_f16, id_bf16, out):
    ctx = ExitStack()
    with ctx:
        def sb(name, shape, dt):
            return ctx.enter_context(nc.sbuf_tensor(name, shape, dt))

        def sem(name):
            return ctx.enter_context(nc.semaphore(name))

        xT = sb("xT", [P, 2, 2, NTOK], F16)
        attT = sb("attT", [P, 2, 2, NTOK], F16)
        W = sb("W", [P, 2, 2, NW], F16)
        wqkv = sb("wqkv", [P, 2, 2, 3 * C], F16)
        wo = sb("wo", [P, 2, 2, C], F16)
        qs = sb("qs", [P, 2, H, T], F16)
        ks = sb("ks", [P, 2, H, T], F16)
        pT = sb("pT", [P, 2, FILLS, 512], F32)
        V = sb("V", [P, 2, 2, VW], F32)
        qk = sb("qk", [P, 4, T], F32)
        qk16 = sb("qk16", [P, 4, 2, T], F16)
        xs = sb("xs", [P, 2, C], F32)
        xn = sb("xn", [P, 2, C], F32)
        x16 = sb("x16", [P, 2, 2, C], F16)
        oT = sb("oT", [P, 2, 512], F32)
        att = sb("att", [P, 2, C], F32)
        att16 = sb("att16", [P, 2, 2, C], F16)
        emb_sb = sb("emb_sb", [P, T], F32)
        mask_q_sb = sb("mask_q_sb", [P, T], F32)
        mask_k_sb = sb("mask_k_sb", [P, 512], BF16)
        idf = sb("idf", [P, P], F32)
        idh = sb("idh", [P, P], F16)
        idb = sb("idb", [P, P], BF16)
        vb = sb("vb", [P, C], F32)
        qb = sb("qb", [P, 4], F32)
        qb16 = sb("qb16", [P, 4], F32)
        stats = sb("stats", [P, 2, 6], F32)
        moments = sb("moments", [P, 2, 2], F32)
        vareps = sb("vareps", [P, 2], F32)
        rstd = sb("rstd", [P, 2], F32)
        half = sb("half", [P, 2], F32)
        mx = sb("mx", [P, 2, 2, H], F32)
        sh16 = sb("sh16", [P, 2, 2, H], F16)
        shT = sb("shT", [2 * H, T], F16)
        rden = sb("rden", [P, 2, H], F32)
        code = sb("code", [P, SW], I32)
        scale = sb("scale", [P, SW], F32)
        sign = sb("sign", [P, 2, SW], I32)
        wbits = sb("wbits", [P, 2, SW], I32)
        all_scales = sign[:, 0, 0:P // 16 * NW // P].bitcast(F32)

        wstage = pT[:, :, :, :].rearrange("p a b c -> p (a b c)")
        wqkv_in = wstage[:, 0:6 * C].rearrange("p (a n) -> p a n", a=2)
        wo_in = wstage[:, 6 * C:8 * C].rearrange("p (a n) -> p a n", a=2)
        qs_f = qs[:, :, :, :].rearrange("p a h t -> p (a h t)")
        ks_f = ks[:, :, :, :].rearrange("p a h t -> p (a h t)").bitcast(F32)
        gel = qs_f[:, 0:2048].bitcast(F32).rearrange("p (b n) -> p b n", b=2)
        inter = qs_f[:, 2048:4096].bitcast(F32).rearrange("p (b n) -> p b n", b=2)
        inter16 = ks_f[:, 0:1024].bitcast(F16).rearrange("p (b s n) -> p b s n", b=2, s=2)
        ob = ks_f[:, 1024:1024 + C]
        xres = ks_f[:, 2048:4096].rearrange("p (b s c) -> p b s c", b=2, s=SUB)
        res = qs_f[:, 4096:8192].bitcast(F32).rearrange("p (b s c) -> p b s c", b=2, s=SUB)

        bank = [ctx.enter_context(nc.psum_tensor(f"bank{n}", [P, 512], F32)) for n in range(8)]
        bT, bP, bPV, bA, bB = bank[0], bank[1], bank[2], bank[3:6], bank[6:8]
        bT16 = bT[:, :].bitcast(F16)
        bG, bU, bOut = [bA[0], bB[0]], [bA[1], bB[1]], [bP, bA[2]]

        ws_scales = nc.dram_tensor("ws_scales", [P // 16, NW], F32).ap()
        stack = nc.dram_tensor("stack", [2, 2, 2, D, H, T], F16).ap()

        const_in, id_in, wts_in, x_in, codes_in = sem("const_in"), sem("id_in"), sem("wts_in"), sem("x_in"), sem("codes_in")
        stack_out = sem("stack_out")
        scales_in, scales_ready, scales_out = sem("scales_in"), sem("scales_ready"), sem("scales_out")
        stack_in = [[sem(f"stack_in{v}{hf}") for hf in range(2)] for v in range(2)]
        shift_in, ob_in = sem("shift_in"), sem("ob_in")
        xres_in = [sem("xres_in0"), sem("xres_in1")]
        out_done = [sem("out_done0"), sem("out_done1")]
        qs_filled, ks_filled, half_ready, v_zero, v_ones, w_high, w_low = (
            sem("qs_filled"), sem("ks_filled"), sem("half_ready"), sem("v_zero"), sem("v_ones"), sem("w_high"), sem("w_low"))
        stats_done, moments_ready, eps_added, rstd_ready = (
            sem("stats_done"), sem("moments_ready"), sem("eps_added"), sem("rstd_ready"))
        xn_ready, x_high, x_low, xT_ready, xT_kept = (
            sem("xn_ready"), sem("x_high"), sem("x_low"), sem("xT_ready"), sem("xT_kept"))
        proj_ready, rope_done, qk_high, qk_low = sem("proj_ready"), sem("rope_done"), sem("qk_high"), sem("qk_low")
        v_ready, v_kept = sem("v_ready"), sem("v_kept")
        scores_ready, max_taken, shift_split = sem("scores_ready"), sem("max_taken"), sem("shift_split")
        shT_ready, shT_kept, rows_zeroed = sem("shT_ready"), sem("shT_kept"), sem("rows_zeroed")
        shifted_ready, exp_done, pv_done, oT_kept = (
            sem("shifted_ready"), sem("exp_done"), sem("pv_done"), sem("oT_kept"))
        o_ready, rden_ready, o_taken, att_high, att_low = (
            sem("o_ready"), sem("rden_ready"), sem("o_taken"), sem("att_high"), sem("att_low"))
        attT_ready, attT_kept = sem("attT_ready"), sem("attT_kept")
        bits_step, bits_ready, wf_ready, wf_high, wf_low = (
            sem("bits_step"), sem("bits_ready"), sem("wf_ready"), sem("wf_high"), sem("wf_low"))
        gate_ready, up_ready, gelu_done, inter_ready, inter_high, inter_low = (
            sem("gate_ready"), sem("up_ready"), sem("gelu_done"), sem("inter_ready"), sem("inter_high"), sem("inter_low"))
        down_done, acc_taken, xres_ready = (
            sem("down_done"), sem("acc_taken"), sem("xres_ready"))

        block = ctx.enter_context(nc.Block())

        FIRST, LOOP, LAST = -4, (3, 11), B + 1

        def pipeline(eng, step):
            def fixed(i):
                step(i, i % 2, lambda lag: 0 <= i + lag < B)
            for i in range(FIRST, LOOP[0]):
                fixed(i)
            with eng.Fori(0, (LOOP[1] - LOOP[0]) // 2) as j:
                for u in (0, 1):
                    step(j * 2 + (LOOP[0] + u), (LOOP[0] + u) % 2, lambda lag: True)
            for i in range(LOOP[1], LAST):
                fixed(i)

        def wait_apart(eng, semaphore, value):
            if not isinstance(value, int):
                value = eng.to_reg(value)
                eng.wait_ge(semaphore, 1)
            eng.wait_ge(semaphore, value)

        def early(i, lag, n):
            return isinstance(i, int) and i + lag < n

        @block.sync
        def _(sp):
            def load_x(b):
                sp.dma_start(xs[:, :, :], x[bass.ds(b * 2, 2)].rearrange("a p c -> p a c")).then_inc(x_in, 16)

            load_x(0)
            sp.dma_start(idh[:, :], id_f16).then_inc(id_in, 16)
            for dst, src in ((qb, qkv_b), (emb_sb, emb), (mask_q_sb, mask_q), (mask_k_sb, mask_k),
                             (idf, id_f32), (idb, id_bf16)):
                sp.dma_start(dst[:, :], src).then_inc(const_in, 16)
            sp.dma_start(vb[:, :], v_b.partition_broadcast(P)).then_inc(const_in, 16)

            def load_stack(b, v, hf):
                if not early(b, 0, 2):
                    sp.wait_ge(shifted_ready, (b - 2) * (GROUPS * FILLS) + 6 * (hf + 1))
                hs = slice(8 * hf, 8 * hf + 8)
                q0 = stack[v, 0, :, :, hs, :]
                k0 = stack[v, 1, :, :, hs, :]
                n = 8 * T
                src = bass.AP(q0.tensor, q0.offset, [[0, 2], [H * T, 2 * D], [1, n]])
                sp.dma_start(qs[0:4 * D, v, hs, :].rearrange("p h t -> p (h t)"), src).then_inc(stack_in[v][hf], 16)
                for part in range(2):
                    src = bass.AP(k0.tensor, k0.offset + part * D * H * T, [[0, 2], [H * T, D], [1, n]])
                    dst = ks[2 * part * D:2 * (part + 1) * D, v, hs, :].rearrange("p h t -> p (h t)")
                    sp.dma_start(dst, src).then_inc(stack_in[v][hf], 16)

            def step(i, u, live):
                if live(-1):
                    sp.wait_ge(shT_kept, i)
                    for part in range(2):
                        r = 4 * D + part
                        sp.dma_start(qs[r:r + 1, 1 - u, :, :], shT[part * H:(part + 1) * H, :]).then_inc(shift_in, 16)
                if live(0) and not early(i, 0, 1):
                    load_stack(i, u, 1)
                if live(4) and not early(i, 0, 1):
                    sp.wait_ge(xn_ready, i + 4)
                    load_x(i + 4)
                if live(0):
                    if not early(i, 0, 1):
                        sp.wait_ge(bits_step, i)
                        sp.wait_ge(wf_ready, i)
                    sp.dma_start(code[:, :], codes[:, bass.ds(i * SW, SW)]).then_inc(codes_in, 16)
                    if early(i, 0, 1):
                        sp.wait_ge(scales_out, 16)
                    s0 = ws_scales[:, bass.ds(i * SW, SW)]
                    src = bass.AP(s0.tensor, s0.offset, [[NW, P // 16], [0, 16], [1, SW]])
                    sp.dma_start(scale[:, :], src).then_inc(codes_in, 16)
                if live(1):
                    sp.wait_ge(stack_out, (i + 2) * 128)
                    load_stack(i + 1, 1 - u, 0)
                    if early(i, 1, 1):
                        load_stack(0, 0, 1)
                        sp.wait_ge(scales_ready, 1)
                        sp.dma_start(ws_scales.rearrange("a (b n) -> (a b) n", b=16), all_scales)\
                          .then_inc(scales_out, 16)
                if live(2):
                    b = i + 2
                    sp.wait_ge(qk_high, b + 1)
                    if not early(i, 2, 2):
                        for hf in range(2):
                            sp.wait_ge(stack_in[u][hf], i * 24 + (48 - 24 * u))
                    for part in range(2):
                        if part == 1:
                            sp.wait_ge(qk_low, b + 1)
                        for f in range(4):
                            h0 = 8 * (f % 2)
                            dst = stack[u, f // 2, part].rearrange("d h t -> h d t")[h0:h0 + 8]
                            sp.dma_start(dst, qk16[:, f, part, :]).then_inc(stack_out, 16)
                if early(i, 0, 0):
                    sp.wait_ge(xn_ready, i + 5)
                    load_x(i + 5)

            pipeline(sp, step)

            sp.wait_ge(pv_done, B * GROUPS)
            sp.dma_start(ob, out_b.partition_broadcast(P)).then_inc(ob_in, 16)
            xc = x.rearrange("(k s) p c -> k p s c", s=SUB)
            oc = out.rearrange("(k s) p c -> k p s c", s=SUB)
            for k in range(2):
                sp.dma_start(xres[:, k], xc[k]).then_inc(xres_in[k], 16)

            def store(k, u):
                sp.wait_ge(acc_taken, (k + 1) * 2)
                sp.dma_start(oc[k] if isinstance(k, int) else oc[bass.ds(k, 1)].rearrange("k p s c -> p (k s) c"),
                             res[:, u]).then_inc(out_done[u], 16)

            with sp.Fori(0, NTOK // CH // 2 - 1) as j:
                for u in range(2):
                    store(j * 2 + u, u)
                    sp.dma_start(xres[:, u], xc[bass.ds(j * 2 + (2 + u), 1)].rearrange("k p s c -> p (k s) c"))\
                      .then_inc(xres_in[u], 16)
            for u in range(2):
                store(NTOK // CH - 2 + u, u)
            for u in range(2):
                sp.wait_ge(out_done[u], NTOK // CH // 2 * 16)

        @block.gpsimd
        def _(pool):
            nc.gpsimd.memset(half[:, :], -0.5).then_inc(half_ready, 1)
            pool.wait_ge(half_ready, 1)
            nc.gpsimd.memset(V[:, :, :, :], 0.0).then_inc(v_zero, 1)
            pool.wait_ge(v_zero, 1)

            def fill_keys(v, n):
                nc.gpsimd.memset(ks[64:128, v, :, :].bitcast(F32), 0.0).then_inc(ks_filled, 1)
                pool.wait_ge(ks_filled, n - 1)
                nc.gpsimd.memset(ks[64:66, v, :, :].bitcast(F32), TWO_ONES).then_inc(ks_filled, 1)
                pool.wait_ge(ks_filled, n)

            def zero_rows(i, u, hf, before):
                pool.wait_ge(*before)
                wait_apart(pool, shifted_ready, (i - 1) * (GROUPS * FILLS) + 6 * (hf + 1))
                nc.gpsimd.memset(qs[64:66, 1 - u, 8 * hf:8 * hf + 8, :].bitcast(F32), 0.0).then_inc(rows_zeroed, 1)
                pool.wait_ge(rows_zeroed, (i - 1) * 2 + hf + 1)

            def x_rstd(i):
                b = i + 4
                wait_apart(pool, moments_ready, b + 1)
                nc.gpsimd.tensor_scalar(vareps[:, :], moments[:, :, 1], EPS, None, ALU.add).then_inc(eps_added, 1)
                pool.wait_ge(eps_added, b + 1)
                if not early(i, 4, 1):
                    pool.wait_ge(xn_ready, b)
                nc.gpsimd.tensor_tensor(rstd[:, :], vareps[:, :], half[:, :], ALU.pow).then_inc(rstd_ready, 1)

            def x_lo(i):
                pool.wait_ge(x_high, i + 5)
                nc.gpsimd.tensor_tensor(x16[:, :, 1, :], xn[:, :, :], x16[:, :, 0, :], ALU.subtract).then_inc(x_low, 1)

            def att_lo(i, qt):
                pool.wait_ge(att_high, (i - 2) * 2 + qt + 1)
                nc.gpsimd.tensor_tensor(att16[:, qt, 1, :], att[:, qt, :], att16[:, qt, 0, :], ALU.subtract)\
                    .then_inc(att_low, 1)

            def step(i, u, live):
                if live(-1):
                    pool.wait_ge(bits_step, i)
                    nc.gpsimd.tensor_tensor(wbits[:, :, :], wbits[:, :, :], sign[:, :, :], ALU.add)\
                        .then_inc(bits_ready, 1)
                    pool.wait_ge(codes_in, i * 32)
                    pool.wait_ge(bits_ready, i)
                    val = wbits[:, :, :].bitcast(F16).rearrange("p a (n e) -> p a n e", e=2)[:, :, :, 0]
                    sc = scale[:, :].unsqueeze(1).broadcast_to([P, 2, SW])
                    nc.gpsimd.tensor_tensor(wbits[:, :, :].bitcast(F32), val, sc, ALU.mult).then_inc(wf_ready, 1)
                if live(2):
                    b = i + 2
                    pool.wait_ge(qk_high, b + 1)
                    if not early(i, 2, 1):
                        pool.wait_ge(stack_out, b * 128)
                    nc.gpsimd.tensor_tensor(qk16[:, :, 1, :], qk[:, :, :], qk16[:, :, 0, :], ALU.subtract)\
                        .then_inc(qk_low, 1)
                if live(4) and not live(0):
                    x_rstd(i)
                    x_lo(i)
                    if early(i, 4, 1):
                        pool.wait_ge(x_low, 1)
                        fill_keys(0, 2)
                    elif early(i, 4, 3) and not early(i, 4, 2):
                        pool.wait_ge(x_low, i + 5)
                        fill_keys(1, 4)
                if live(1) and not early(i, 1, 2):
                    zero_rows(i, u, 0, (qk_low, i + 3) if live(2) else (wf_ready, i))
                if live(-2):
                    att_lo(i, 0)
                if live(0) and live(4):
                    x_rstd(i)
                if live(-2):
                    att_lo(i, 1)
                if live(-1):
                    pool.wait_ge(wf_high, i)
                    o = bass.ds((i - 1) * SW, SW)
                    nc.gpsimd.tensor_tensor(W[:, :, 1, o], wbits[:, :, :].bitcast(F32), W[:, :, 0, o], ALU.subtract)\
                        .then_inc(wf_low, 1)
                if live(0) and live(4):
                    x_lo(i)
                if live(1) and not early(i, 1, 2):
                    zero_rows(i, u, 1, (x_low, i + 5) if live(4) else (wf_low, i))

            pipeline(pool, step)
            for qt in range(2):
                att_lo(B + 1, qt)

            pool.wait_ge(ob_in, 16)

            def residual(k, u):
                pool.wait_ge(xres_in[u], (k // 2 + 1) * 16 if isinstance(k, int) else (k + 1) * 16)
                nc.gpsimd.tensor_tensor(xres[:, u], xres[:, u], ob.unsqueeze(1).broadcast_to([P, SUB, C]), ALU.add)\
                    .then_inc(xres_ready, 1)

            with pool.Fori(0, NTOK // CH // 2) as j:
                for u in range(2):
                    residual(j + 0, u)

        @block.scalar
        def _(act):
            act.dma_start(wqkv_in, qkv_wT).then_inc(wts_in, 16)
            act.dma_start(wo_in, out_wT).then_inc(wts_in, 16)
            act.dma_start(all_scales, scales.rearrange("a (b n) -> (a b) n", b=16)).then_inc(scales_in, 16)

            def exps(i, first, last):
                b = i - 1
                for m in range(first, last):
                    g, f = m // FILLS, m % FILLS
                    if f == 0:
                        if g < 2 and early(i, -1, 1):
                            act.wait_ge(w_low, 3)
                        else:
                            act.wait_ge(pv_done, b * GROUPS + g - 1)
                    act.wait_ge(shifted_ready, b * (GROUPS * FILLS) + m + 1)
                    nc.scalar.activation(pT[:, g % 2, f, :], bB[m % len(bB)][:, :], ACT.Exp, scale=D ** -0.5)\
                        .then_inc(exp_done, 1)

            def keep_o(b, hf):
                act.wait_ge(pv_done, b * GROUPS + 2 * hf + 2)
                if not early(b, 0, 1):
                    act.wait_ge(o_ready, b * 2)
                nc.scalar.activation(oT[:, hf, :], bPV[:, :], ACT.Copy).then_inc(oT_kept, 1)

            def x_hi(i):
                b = i + 4
                act.wait_ge(xn_ready, b + 1)
                if not early(i, 4, 1):
                    act.wait_ge(xT_ready, b)
                nc.scalar.activation(x16[:, :, 0, :], xn[:, :, :], ACT.Copy).then_inc(x_high, 1)

            def att_hi(i, qt):
                b = i - 2
                act.wait_ge(o_taken, b * 2 + qt + 1)
                if not early(i, -2, 1):
                    act.wait_ge(attT_ready, b)
                nc.scalar.activation(att16[:, qt, 0, :], att[:, qt, :], ACT.Copy).then_inc(att_high, 1)

            def keep_attT(i):
                act.wait_ge(attT_ready, i - 1)
                nc.scalar.activation(attT[:, :, :, bass.ds((i - 2) * T, T)].rearrange("p a s t -> p (a s) t"),
                                     bT16.rearrange("p (a t) -> p a t", a=4), ACT.Copy).then_inc(attT_kept, 1)

            def keep_xT(i):
                b = i + 3
                act.wait_ge(xT_ready, b + 1)
                nc.scalar.activation(xT[:, :, :, bass.ds(b * T, T)].rearrange("p a s t -> p (a s) t"),
                                     bT16.rearrange("p (a t) -> p a t", a=4), ACT.Copy).then_inc(xT_kept, 1)

            def qk_hi(i):
                b = i + 2
                act.wait_ge(rope_done, (b + 1) * 2)
                if not early(i, 2, 1):
                    act.wait_ge(stack_out, b * 128)
                nc.scalar.activation(qk16[:, :, 0, :], qk[:, :, :], ACT.Copy).then_inc(qk_high, 1)

            def weights_hi(i):
                act.wait_ge(wf_ready, i)
                nc.scalar.activation(W[:, :, 0, bass.ds((i - 1) * SW, SW)], wbits[:, :, :].bitcast(F32), ACT.Copy)\
                    .then_inc(wf_high, 1)

            def keep_shT(i):
                act.wait_ge(shT_ready, i + 1)
                if not early(i, 0, 1):
                    act.wait_ge(shift_in, i * 32)
                nc.scalar.activation(shT[:, :], bT16[0:2 * H, 0:T], ACT.Copy).then_inc(shT_kept, 1)

            def step(i, u, live):
                if isinstance(i, int) and i == FIRST + 1:
                    act.wait_ge(wts_in, 32)
                    nc.scalar.activation(wqkv[:, :, 0, :], wqkv_in, ACT.Copy, scale=WS).then_inc(w_high, 1)
                    nc.scalar.activation(wo[:, :, 0, :], wo_in, ACT.Copy, scale=WS).then_inc(w_high, 1)
                if live(-1):
                    keep_shT(i - 1)
                if live(-2):
                    keep_o(i - 2, 1)
                if live(-1):
                    exps(i, 0, 1)
                if live(3):
                    keep_xT(i)
                if live(-1):
                    exps(i, 1, 3)
                if live(2):
                    qk_hi(i)
                if live(4) and not live(0):
                    x_hi(i)
                if live(-1):
                    exps(i, 3, 5)
                    weights_hi(i)
                    exps(i, 5, 7)
                if live(-2):
                    att_hi(i, 0)
                if live(-1):
                    exps(i, 7, 8)
                    keep_o(i - 1, 0)
                    exps(i, 8, 9)
                if live(-2):
                    att_hi(i, 1)
                if live(-1):
                    exps(i, 9, 10)
                if live(0) and live(4):
                    x_hi(i)
                if live(-1):
                    exps(i, 10, 11)
                if live(-2):
                    keep_attT(i)
                if live(-1):
                    exps(i, 11, 12)

            pipeline(act, step)

            def mlp(n, v):
                act.wait_ge(gate_ready, n + 1)
                if not (isinstance(n, int) and n < 2):
                    act.wait_ge(inter_ready, n - 1)
                nc.scalar.activation(gel[:, v], bG[v][:, :], ACT.Gelu_apprx_tanh, scale=1.0 / WS).then_inc(gelu_done, 1)
                act.wait_ge(inter_ready, n + 1)
                if not (isinstance(n, int) and n < 2):
                    act.wait_ge(down_done, n - 1)
                nc.scalar.activation(inter16[:, v, 0, :], inter[:, v, :], ACT.Copy).then_inc(inter_high, 1)

            keep_o(B - 1, 1)
            mlp(0, 0)
            att_hi(B + 1, 0)
            mlp(1, 1)
            att_hi(B + 1, 1)
            mlp(2, 0)
            mlp(3, 1)
            keep_attT(B + 1)
            with act.Fori(0, NTOK // CH * NTILES // 2 - 2) as j:
                for v in range(2):
                    mlp(j * 2 + (4 + v), v)

        @block.vector
        def _(dve):
            nc.vector.memset(qs[64:128, 0, :, :].bitcast(F32), 0.0).then_inc(qs_filled, 1)

            def prepare():
                nc.vector.memset(qs[64:128, 1, :, :].bitcast(F32), 0.0).then_inc(qs_filled, 1)
                dve.wait_ge(w_high, 1)
                nc.vector.scalar_tensor_tensor(out=wqkv[:, :, 1, :], in0=wqkv_in, scalar=WS, in1=wqkv[:, :, 0, :],
                                               op0=ALU.mult, op1=ALU.subtract).then_inc(w_low, 1)
                dve.wait_ge(const_in, 7 * 16)
                nc.vector.tensor_scalar(qb16[:, :], qb[:, :], WS, None, ALU.mult).then_inc(w_low, 1)
                dve.wait_ge(scales_in, 16)
                nc.vector.tensor_scalar(all_scales, all_scales, CODE * WS, None, ALU.mult)\
                    .then_inc(scales_ready, 1)
                dve.wait_ge(w_high, 2)
                nc.vector.scalar_tensor_tensor(out=wo[:, :, 1, :], in0=wo_in, scalar=WS, in1=wo[:, :, 0, :],
                                               op0=ALU.mult, op1=ALU.subtract).then_inc(w_low, 1)
                dve.wait_ge(w_low, 2)
                dve.wait_ge(v_zero, 1)
                for a in range(2):
                    for kt in range(2):
                        nc.vector.memset(V[:, a, kt, D:D + (H - 1) * HP + 1:HP], 1.0).then_inc(v_ones, 1)

            def rope(i, pair):
                b = i + 2
                dve.wait_ge(proj_ready, b * 2 + pair + 1)
                if pair == 0 and not early(i, 2, 1):
                    dve.wait_ge(qk_low, b)
                for n in range(2):
                    f = 2 * pair + n
                    last = nc.vector.scalar_tensor_tensor(
                        out=qk[:, f, :], in0=bP[:, n * T:(n + 1) * T], scalar=qb16[:, f:f + 1], in1=emb_sb[:, :],
                        op0=ALU.add, op1=ALU.mult)
                last.then_inc(rope_done, 1)

            def x_stats(i):
                b = i + 4
                dve.wait_ge(x_in, (b + 1) * 16)
                for tt in range(2):
                    last = nc.vector.bn_stats(stats[:, tt, :], xs[:, tt, :])
                last.then_inc(stats_done, 1)

            def x_moments(i):
                wait_apart(dve, stats_done, i + 5)
                for tt in range(2):
                    last = nc.vector.bn_aggr(moments[:, tt, :], stats[:, tt, :])
                last.then_inc(moments_ready, 1)

            def x_scale(i):
                b = i + 4
                dve.wait_ge(rstd_ready, b + 1)
                if not early(i, 4, 1):
                    dve.wait_ge(x_low, b)
                for tt in range(2):
                    last = nc.vector.tensor_scalar(xn[:, tt, :], xs[:, tt, :], moments[:, tt, 0:1],
                                                   rstd[:, tt:tt + 1], ALU.subtract, ALU.mult)
                last.then_inc(xn_ready, 1)

            def row_max(i, u, first, last_fill):
                for m in range(first, last_fill):
                    g, f = m // FILLS, m % FILLS
                    wait_apart(dve, scores_ready, i * (GROUPS * FILLS) + m + 1)
                    s = bA[m % len(bA)]
                    for n in range(HEADS if f == 0 else 2):
                        if f == 0:
                            h, qt, w = HEADS * g + n, 0, P
                        else:
                            h, qt, w = HEADS * g + 2 * (f - 1) + n, 1, T
                        last = nc.vector.tensor_tensor_reduce(
                            s[:, n * w:(n + 1) * w], s[:, n * w:(n + 1) * w], mask_q_sb[:, T - w:T], 1.0, -3e38,
                            ALU.add, ALU.max, mx[:, u, qt, h:h + 1])
                    last.then_inc(max_taken, 1)

            def normalise(i, qt):
                b = i - 2
                dve.wait_ge(o_ready, b * 2 + qt + 1)
                o = bT[:, :].rearrange("p (h e) -> p h e", e=32)
                nc.vector.reciprocal(rden[:, qt, :], o[:, :, D]).then_inc(rden_ready, 1)
                dve.wait_ge(rden_ready, b * 2 + qt + 1)
                if not early(i, -2, 1):
                    dve.wait_ge(att_low, (b - 1) * 2 + qt + 1)
                nc.vector.tensor_tensor(att[:, qt, :].rearrange("p (h d) -> p h d", d=D), o[:, :, 0:D],
                                        rden[:, qt, :].unsqueeze(2).broadcast_to([P, H, D]), ALU.mult)\
                    .then_inc(o_taken, 1)

            def keep_v(i, u):
                dve.wait_ge(v_ready, i + 1)
                if not early(i, 0, 2):
                    dve.wait_ge(pv_done, (i - 1) * GROUPS)
                for kt in range(2):
                    dst = V[:, u, kt, 0:H * HP].rearrange("p (h e) -> p h e", e=HP)[:, :, 0:D]
                    last = nc.vector.scalar_tensor_tensor(
                        out=dst, in0=bP[:, kt * C:(kt + 1) * C].rearrange("p (h d) -> p h d", d=D),
                        scalar=1.0 / WS, in1=vb[:, :].rearrange("p (h d) -> p h d", d=D), op0=ALU.mult, op1=ALU.add)
                last.then_inc(v_kept, 1)

            def shift(i, u):
                dve.wait_ge(max_taken, (i + 1) * (GROUPS * FILLS))
                if not early(i, 0, 1):
                    dve.wait_ge(shT_ready, i)
                nc.vector.tensor_scalar(sh16[:, :, 0, :], mx[:, u, :, :], -1.0, None, ALU.mult).then_inc(shift_split, 1)
                dve.wait_ge(shift_split, i * 2 + 1)
                nc.vector.scalar_tensor_tensor(out=sh16[:, :, 1, :], in0=mx[:, u, :, :], scalar=-1.0,
                                               in1=sh16[:, :, 0, :], op0=ALU.mult, op1=ALU.subtract)\
                    .then_inc(shift_split, 1)

            def code_bits(i):
                dve.wait_ge(codes_in, (i + 1) * 32)
                if not early(i, 0, 1):
                    dve.wait_ge(wf_low, i)
                for par, (m, s) in enumerate(((0x7, 9), (0x70, 5))):
                    nc.vector.tensor_scalar(wbits[:, par, :], code[:, :], m, s, ALU.bitwise_and,
                                            ALU.logical_shift_left)
                    last = nc.vector.tensor_scalar(sign[:, par, :], code[:, :], (8, 128)[par], (12, 8)[par],
                                                   ALU.bitwise_and, ALU.logical_shift_left)
                last.then_inc(bits_step, 1)

            def step(i, u, live):
                if isinstance(i, int) and i == FIRST + 1:
                    prepare()
                if live(2):
                    rope(i, 0)
                elif live(0):
                    keep_v(i, u)
                if live(0):
                    row_max(i, u, 0, 3)
                if live(2):
                    rope(i, 1)
                if live(4) and not live(0):
                    x_stats(i)
                    x_moments(i)
                if live(0):
                    row_max(i, u, 3, 5)
                if live(0) and live(4):
                    x_stats(i)
                if live(0) and live(2):
                    keep_v(i, u)
                if live(0):
                    row_max(i, u, 5, 6)
                if live(-2):
                    normalise(i, 0)
                if live(0):
                    row_max(i, u, 6, 7)
                if live(0) and live(4):
                    x_moments(i)
                if live(0):
                    row_max(i, u, 7, 9)
                if live(-2):
                    normalise(i, 1)
                if live(4):
                    x_scale(i)
                if live(0):
                    row_max(i, u, 9, 12)
                    shift(i, u)
                    code_bits(i)

            pipeline(dve, step)

            def hidden(n, v):
                dve.wait_ge(gelu_done, n + 1)
                dve.wait_ge(up_ready, n + 1)
                if not (isinstance(n, int) and n < 2):
                    dve.wait_ge(inter_low, n - 1)
                nc.vector.scalar_tensor_tensor(out=inter[:, v, :], in0=bU[v][:, :], scalar=1.0 / WS, in1=gel[:, v],
                                               op0=ALU.mult, op1=ALU.mult).then_inc(inter_ready, 1)
                dve.wait_ge(inter_high, n + 1)
                nc.vector.tensor_tensor(inter16[:, v, 1, :], inter[:, v, :], inter16[:, v, 0, :], ALU.subtract)\
                    .then_inc(inter_low, 1)

            def finish(k, u, stores):
                dve.wait_ge(down_done, (k + 1) * NTILES)
                dve.wait_ge(xres_ready, k + 1)
                if stores is not None:
                    dve.wait_ge(out_done[u], stores)
                for a in range(2):
                    nc.vector.scalar_tensor_tensor(
                        out=res[:, u, 2 * a:2 * a + 2, :], in0=bOut[a][:, :].rearrange("p (s c) -> p s c", s=2),
                        scalar=1.0 / WS, in1=xres[:, u, 2 * a:2 * a + 2, :], op0=ALU.mult, op1=ALU.add)\
                        .then_inc(acc_taken, 1)

            def chunk(k, u, head, stores):
                if head:
                    hidden(0, 0)
                    normalise(B + 1, 0)
                else:
                    hidden(k * NTILES, 0)
                    finish(k - 1, 1 - u, stores)
                for n in range(1, NTILES):
                    hidden(k * NTILES + n, n % 2)
                    if head and n == 1:
                        normalise(B + 1, 1)

            chunk(0, 0, True, None)
            chunk(1, 1, False, None)
            chunk(2, 0, False, None)
            with dve.Fori(0, (NTOK // CH - 4) // 2) as j:
                for u in range(2):
                    chunk(j * 2 + (3 + u), 1 - u, False, (j + 1) * 16)
            chunk(NTOK // CH - 1, 1, False, (NTOK // CH // 2 - 1) * 16)
            finish(NTOK // CH - 1, 1, (NTOK // CH // 2 - 1) * 16)

        @block.tensor
        def _(pe):
            mm = nc.tensor.matmul

            def three(dst, lhs, rhs, start, stop):
                terms = [(a, pl, pr) for a in range(2) for pl, pr in ((0, 0), (0, 1), (1, 0))]
                for n, (a, pl, pr) in enumerate(terms):
                    last = mm(dst, lhs(a, pl), rhs(a, pr), start=start and n == 0,
                              stop=stop and n == len(terms) - 1, skip_group_check=True)
                return last

            def transpose_x(i):
                b = i + 3
                pe.wait_ge(x_high, b + 1)
                pe.wait_ge(x_low, b + 1)
                if not early(i, -1, 0):
                    pe.wait_ge(shT_kept, i)
                if not early(i, 3, 1):
                    pe.wait_ge(xT_kept, b)
                for tt in range(2):
                    for a in range(2):
                        for part in range(2):
                            col = (2 * a + part) * T + tt * P
                            last = nc.tensor.transpose(bT16[:, col:col + P], x16[:, tt, part, a:C:2], idh[:, :])
                last.then_inc(xT_ready, 1)

            def project_qk(i, pair):
                b = i + 2
                if pair == 0:
                    pe.wait_ge(xT_kept, b + 1)
                    if early(i, 2, 1):
                        pe.wait_ge(w_low, 1)
                        pe.wait_ge(const_in, 7 * 16)
                    if not early(i, -1, 0):
                        pe.wait_ge(v_kept, i)
                    elif not early(i, 2, 1):
                        pe.wait_ge(rope_done, b * 2)
                else:
                    pe.wait_ge(rope_done, b * 2 + 1)
                tok = bass.ds(b * T, T)
                for n in range(2):
                    f = 2 * pair + n
                    last = three(bP[:, n * T:(n + 1) * T], lambda a, s: wqkv[:, a, s, f * P:(f + 1) * P],
                                 lambda a, s: xT[:, a, s, tok], n == 0, True)
                last.then_inc(proj_ready, 1)

            def project_v(i, proj_live):
                if proj_live:
                    pe.wait_ge(rope_done, (i + 3) * 2)
                else:
                    pe.wait_ge(v_kept, i)
                for kt in range(2):
                    last = three(bP[:, kt * C:(kt + 1) * C], lambda a, s: xT[:, a, s, bass.ds(i * T + kt * P, P)],
                                 lambda a, s: wqkv[:, a, s, 2 * C:3 * C], kt == 0, True)
                last.then_inc(v_ready, 1)

            def transpose_shift(i):
                pe.wait_ge(shift_split, i * 2 + 2)
                if early(i, -2, 0):
                    pe.wait_ge(xT_kept, i + 4)
                else:
                    pe.wait_ge(attT_kept, i - 1)
                for qt in range(2):
                    last = nc.tensor.transpose(bT16[0:2 * H, qt * P:(qt + 1) * P],
                                               sh16[:, qt, :, :].rearrange("p s h -> p (s h)"), idh[:, :])
                last.then_inc(shT_ready, 1)

            def free_bank(taken, n0, k, ring):
                if not (isinstance(n0, int) and n0 + k < len(ring)):
                    pe.wait_ge(taken, n0 + (k + 1 - len(ring)))

            def scores(i, u, m):
                g, f = m // FILLS, m % FILLS
                if m % 6 == 0:
                    hf = m // 6
                    pe.wait_ge(stack_in[u][hf], i * 24 + (48 - 24 * u))
                    if not early(i, 0, 2):
                        pe.wait_ge(rows_zeroed, (i - 2) * 2 + hf + 1)
                    elif m == 0:
                        pe.wait_ge(qs_filled, 2)
                        pe.wait_ge(ks_filled, 4)
                free_bank(max_taken, i * (GROUPS * FILLS), m, bA)
                dst = bA[m % len(bA)]
                for n in range(HEADS if f == 0 else 2):
                    h = HEADS * g + (n if f == 0 else 2 * (f - 1) + n)
                    w = P if f == 0 else T
                    last = mm(dst[:, n * w:(n + 1) * w], qs[:, u, h, T - P if f else 0:T if f else P],
                              ks[:, u, h, 0:w], start=True, stop=True)
                last.then_inc(scores_ready, 1)

            def shifted(i, u, m):
                g, f = m // FILLS, m % FILLS
                v = 1 - u
                if m == 0:
                    pe.wait_ge(shift_in, i * 32)
                free_bank(exp_done, (i - 1) * (GROUPS * FILLS), m, bB)
                dst = bB[m % len(bB)]
                if f < 2:
                    diag = dst[:, :].rearrange("p (h t) -> p h t", h=2)[:, :, 0:P]
                    mm(diag, idb[:, :], mask_k_sb[:, 0:2 * P], start=True, stop=False, skip_group_check=True)
                else:
                    mm(dst[:, :], idb[:, :], mask_k_sb[:, :], start=True, stop=False, skip_group_check=True)
                for n in range(2 if f < 2 else HEADS):
                    h = HEADS * g + (2 * f + n if f < 2 else n)
                    w = T if f < 2 else P
                    kt = 0 if f < 2 else 1
                    last = mm(dst[:, n * w:(n + 1) * w], ks[:, v, h, kt * P:(kt + 1) * P], qs[:, v, h, T - w:T],
                              start=False, stop=True, skip_group_check=True)
                last.then_inc(shifted_ready, 1)

            def values(b, v, g):
                pe.wait_ge(exp_done, (b * GROUPS + g + 1) * FILLS)
                if g == 0:
                    pe.wait_ge(v_kept, b + 1)
                    if early(b, 0, 1):
                        pe.wait_ge(v_ones, 4)
                if g % 2 == 0 and not (early(b, 0, 1) and g == 0):
                    pe.wait_ge(oT_kept, b * 2 + g // 2)
                c0 = (g % 2) * T
                for n in range(HEADS):
                    h = HEADS * g + n
                    rows = slice(32 * n, 32 * n + 32)
                    p0 = pT[:, g % 2, n // 2, (n % 2) * T:(n % 2 + 1) * T]
                    mm(bPV[rows, c0:c0 + T], V[:, v, 0, h * HP:h * HP + 32], p0, start=True, stop=False,
                       skip_group_check=True)
                for n in range(HEADS):
                    h = HEADS * g + n
                    rows = slice(32 * n, 32 * n + 32)
                    p1 = pT[:, g % 2, 2, n * P:(n + 1) * P]
                    last = mm(bPV[rows, c0 + P:c0 + T], V[:, v, 1, h * HP:h * HP + 32], p1, start=False, stop=True,
                              skip_group_check=True)
                last.then_inc(pv_done, 1)

            def transpose_o(i, qt):
                b = i - 2
                if qt == 0:
                    pe.wait_ge(oT_kept, b * 2 + 2)
                    if early(i, 3, B) or not isinstance(i, int):
                        pe.wait_ge(xT_kept, i + 4)
                    elif i <= B:
                        pe.wait_ge(shT_kept, i)
                    else:
                        pe.wait_ge(attT_kept, b)
                else:
                    pe.wait_ge(o_taken, b * 2 + 1)
                for g in range(GROUPS):
                    c0 = (g % 2) * T + qt * P
                    last = nc.tensor.transpose(bT[:, g * P:(g + 1) * P], oT[:, g // 2, c0:c0 + P], idf[:, :])
                last.then_inc(o_ready, 1)

            def transpose_att(i):
                b = i - 2
                pe.wait_ge(att_high, b * 2 + 2)
                pe.wait_ge(att_low, b * 2 + 2)
                for qt in range(2):
                    for a in range(2):
                        for part in range(2):
                            col = (2 * a + part) * T + qt * P
                            last = nc.tensor.transpose(bT16[:, col:col + P], att16[:, qt, part, a * P:(a + 1) * P],
                                                       idh[:, :])
                last.then_inc(attT_ready, 1)

            def tile_cols(kind, n):
                return slice(kind * HID + n * P, kind * HID + (n + 1) * P)

            def gate_up(k, n):
                t0 = k * NTILES + n
                tok = bass.ds(k * CH, CH)
                v = n % 2
                if not (isinstance(k, int) and t0 < 2):
                    pe.wait_ge(gelu_done, t0 - 1)
                three(bG[v][:, :], lambda a, s: W[:, a, s, tile_cols(0, n)], lambda a, s: xT[:, a, s, tok], True, True)\
                    .then_inc(gate_ready, 1)
                if not (isinstance(k, int) and t0 < 2):
                    pe.wait_ge(inter_ready, t0 - 1)
                three(bU[v][:, :], lambda a, s: W[:, a, s, tile_cols(1, n)], lambda a, s: xT[:, a, s, tok], True, True)\
                    .then_inc(up_ready, 1)

            def project_out(k, halves):
                if isinstance(k, int) and k == 0:
                    pe.wait_ge(attT_kept, CH // T)
                    pe.wait_ge(v_kept, B)
                else:
                    pe.wait_ge(attT_kept, B)
                    pe.wait_ge(acc_taken, k * 2)
                for s4 in [s4 for a in halves for s4 in (2 * a, 2 * a + 1)]:
                    dst = bOut[s4 // 2][:, (s4 % 2) * C:(s4 % 2 + 1) * C]
                    three(dst, lambda a, s: attT[:, a, s, bass.ds(k * CH + s4 * P, P)], lambda a, s: wo[:, a, s, :],
                          s4 % 2 == 0, False)

            def down(k, n):
                t0 = k * NTILES + n
                v = n % 2
                pe.wait_ge(inter_high, t0 + 1)
                pe.wait_ge(inter_low, t0 + 1)
                j, par = n // 2, n % 2
                cols = slice(2 * HID + j * C, 2 * HID + (j + 1) * C)
                for s4 in range(SUB):
                    dst = bOut[s4 // 2][:, (s4 % 2) * C:(s4 % 2 + 1) * C]
                    for pl, pr in ((0, 0), (0, 1), (1, 0)):
                        last = mm(dst, inter16[:, v, pl, s4 * P:(s4 + 1) * P], W[:, par, pr, cols],
                                  start=False, stop=n == NTILES - 1, skip_group_check=True)
                last.then_inc(down_done, 1)
                return last

            def step(i, u, live):
                do = {"A": (0, scores), "S": (-1, shifted), "V": (-1, lambda i, u, g: values(i - 1, 1 - u, g))}

                def run(order):
                    for item in order.split():
                        lag, unit = do[item[0]]
                        if live(lag):
                            unit(i, u, int(item[1:]))

                last_step = isinstance(i, int) and i == B
                if live(2):
                    project_qk(i, 0)
                elif live(0):
                    project_v(i, False)
                if live(-1):
                    transpose_shift(i - 1)
                run("A0")
                if live(-2):
                    values(i - 2, u, GROUPS - 1)
                if last_step:
                    pe.wait_ge(wf_low, -(-2 * HID // SW))
                    pe.wait_ge(wf_high, -(-2 * HID // SW))
                    pe.wait_ge(max_taken, B * GROUPS * FILLS)
                    gate_up(0, 0)
                run("A1 A2")
                if live(0) and live(3):
                    transpose_x(i)
                if live(2):
                    project_qk(i, 1)
                if live(3) and not live(0):
                    transpose_x(i)
                run("A3 S0 S1 A4 S2")
                if live(0) and live(2):
                    project_v(i, True)
                run("S3 A5 S4")
                if live(-2):
                    transpose_o(i, 0)
                run("A6 S5 V0 A7 S6")
                if last_step:
                    project_out(0, (0,))
                run("V1 A8 S7")
                if live(-2):
                    transpose_o(i, 1)
                run("S8 A9 A10 S9 A11")
                run("V2 S10")
                if live(-2):
                    transpose_att(i)
                run("S11")

            pe.wait_ge(id_in, 16)
            pipeline(pe, step)

            project_out(0, (1,))
            values(B - 1, (B - 1) % 2, GROUPS - 1)
            pe.wait_ge(exp_done, B * GROUPS * FILLS)
            gate_up(0, 1)
            transpose_o(B + 1, 0)
            pe.wait_ge(wf_low, SLICES - 1)
            pe.wait_ge(wf_high, SLICES - 1)
            down(0, 0)
            gate_up(0, 2)
            transpose_o(B + 1, 1)
            down(0, 1)
            gate_up(0, 3)
            transpose_att(B + 1)
            pe.wait_ge(wf_low, SLICES)
            pe.wait_ge(wf_high, SLICES)
            for n in range(4, NTILES):
                down(0, n - 2)
                gate_up(0, n)
            down(0, NTILES - 2)

            with pe.Fori(0, NTOK // CH - 1) as j:
                k = j + 1
                gate_up(k, 0)
                down(k - 1, NTILES - 1)
                gate_up(k, 1)
                project_out(k, (0, 1))
                for n in range(2, NTILES):
                    down(k, n - 2)
                    gate_up(k, n)
                down(k, NTILES - 2)
            down(NTOK // CH - 1, NTILES - 1)


def kernel(L0_attn_x, L0_attn_qkv_w, L0_attn_qkv_b, L0_attn_out_w, L0_attn_out_b, L0_ffn_gate_W_packed,
           L0_ffn_gate_scales, L0_ffn_up_W_packed, L0_ffn_up_scales, L0_ffn_down_W_packed, L0_ffn_down_scales):
    import concourse.bacc as bacc
    import ml_dtypes
    from concourse.bass_utils import run_bass_kernel_spmd

    a = np.asarray

    def even_odd_rows(w):
        return a(w).T.reshape(P, 2, -1)

    def hidden_order(w):
        return a(w).reshape(HID // (2 * P), P, 2, -1).transpose(3, 0, 2, 1).reshape(-1, HID)

    def down_order(w, p):
        return a(w).reshape(C, -1, p).transpose(2, 1, 0).reshape(p, -1)

    t = np.arange(T, dtype=np.float32)[:, None]
    angle = (t * (np.arange(0, D, 2, dtype=np.float32) / np.float32(D))[None, :]).astype(np.float64)
    emb = np.concatenate([np.sin(angle), np.cos(angle)], axis=-1).astype(np.float32)
    q, k = np.arange(P)[:, None], np.arange(P)[None, :]
    tri = np.where(k > q, np.float32(NEG), np.float32(0))
    arrays = {
        "x": a(L0_attn_x).reshape(NTOK // P, P, C),
        "qkv_wT": even_odd_rows(L0_attn_qkv_w),
        "qkv_b": a(L0_attn_qkv_b)[:2 * C].reshape(4, P).T,
        "v_b": a(L0_attn_qkv_b)[2 * C:],
        "out_wT": a(L0_attn_out_w).T.reshape(2, P, C).transpose(1, 0, 2),
        "out_b": a(L0_attn_out_b),
        "codes": np.concatenate([hidden_order(L0_ffn_gate_W_packed), hidden_order(L0_ffn_up_W_packed),
                                 down_order(L0_ffn_down_W_packed, P)], axis=1),
        "scales": np.concatenate([hidden_order(L0_ffn_gate_scales), hidden_order(L0_ffn_up_scales),
                                  down_order(L0_ffn_down_scales, P // 16)], axis=1),
        "emb": np.tile(emb.T / np.float32(WS), (P // D, 1)),
        "mask_q": np.concatenate([np.zeros((P, P), np.float32), tri], axis=1),
        "mask_k": np.tile(tri.T, (1, 4)).astype(ml_dtypes.bfloat16),
        "id_f32": np.eye(P, dtype=np.float32),
        "id_f16": np.eye(P, dtype=np.float16),
        "id_bf16": np.eye(P, dtype=ml_dtypes.bfloat16),
    }
    arrays = {f"in_{n}": np.ascontiguousarray(v) for n, v in arrays.items()}
    nc = bacc.Bacc("TRN2", target_bir_lowering=False, num_devices=1)
    aps = [nc.dram_tensor(n, v.shape, mybir.dt.from_np(v.dtype), kind="ExternalInput").ap() for n, v in arrays.items()]
    out = nc.dram_tensor("out", (NTOK // P, P, C), F32, kind="ExternalOutput").ap()
    build(nc, *aps, out)
    r = run_bass_kernel_spmd(nc, [arrays], core_ids=[0])
    return r.results[0]["out"].reshape(B, T, C)
```
